# Optimizing a Trainium2 kernel written in Bass

```python
import numpy as np
import jax
import jax.numpy as jnp

def _softmax(x, axis=-1):
    return jax.nn.softmax(x, axis=axis)

def _gelu(x):
    return jax.nn.gelu(x, approximate=True)

def _silu(x):
    return jax.nn.silu(x)

def _sigmoid(x):
    return jax.nn.sigmoid(x)

def _layernorm(x, axis=-1, eps=1e-05):
    m = jnp.mean(x, axis=axis, keepdims=True)
    v = jnp.var(x, axis=axis, keepdims=True)
    return (x - m) / jnp.sqrt(v + eps)

def _scatter_add(tgt, idx, src, axis=0):
    return tgt.at[idx].add(src)

def _segment_sum(src, seg, n):
    return jax.ops.segment_sum(src, seg, n)
kernel_name = 'mk_perceiver_d1_seqx_r2_f409d2'

def setup_inputs(seed: int=0):
    np.random.seed(seed)
    _w = jnp.asarray

    def _rec_inputs():
        import jax
        import jax.numpy as jnp
        _rk = jax.random.key(seed)
        x = -0.000125 + 0.9999 * jax.random.normal(jax.random.fold_in(_rk, 1), (32, 32, 1024), jnp.float32)
        _lenS = 32 - jax.random.randint(jax.random.fold_in(_rk, 7), (32,), 0, max(1, 32 // 4) + 1, jnp.int32)
        _lenS2 = 257 - jax.random.randint(jax.random.fold_in(_rk, 8), (32,), 0, max(1, 257 // 4) + 1, jnp.int32)
        _ctx_2048P = jax.random.normal(jax.random.fold_in(_rk, 11), (32, 16, 1024), jnp.float32)
        _ctx_2048c = jax.random.dirichlet(jax.random.fold_in(_rk, 511), 0.3 * jnp.ones((16,), jnp.float32), (32, 257))
        _ctx_2048t = jnp.einsum('bsk,bkd->bsd', _ctx_2048c, _ctx_2048P)
        _ctx_2048t = _ctx_2048t * jax.lax.rsqrt(jnp.mean(jnp.square(_ctx_2048t)) + 1e-12) * 0.953939
        ctx_2048 = -0.000514642 + 1.00011 * (_ctx_2048t + 0.3 * jax.random.normal(jax.random.fold_in(_rk, 611), (32, 257, 1024), jnp.float32))
        _validS = jnp.arange(32)[None, :] < _lenS[:, None]
        _validS2 = jnp.arange(257)[None, :] < _lenS2[:, None]
        _causal = jnp.tril(jnp.ones((32, 32), dtype=bool))
        mask_BxS2_bk0 = jnp.logical_not(jnp.broadcast_to(_validS2[:, :], (32, 257)))
        return (x, ctx_2048, mask_BxS2_bk0)
    x, ctx_2048, mask_BxS2_bk0 = _rec_inputs()

    def _L0_xattn_setup():
        import jax, jax.numpy as jnp
        import numpy as np
        key = jax.random.key(seed)
        k1, k2, k3 = jax.random.split(key, 3)
        B, S, D, M = (8, 1024, 1024, 128)
        hidden_states = jax.random.normal(k1, (B, S, D), dtype=jnp.float32)
        memory_tokens = jax.random.normal(k2, (B, M, D), dtype=jnp.float32)
        memory_mask = jax.random.randint(k3, (B, M), 0, 2).astype(jnp.bool_)
        return {'hidden_states': hidden_states, 'memory_tokens': memory_tokens, 'memory_mask': memory_mask}
    _L0_xattn_all = _L0_xattn_setup()
    _L0_xattn_in = {k: v for k, v in _L0_xattn_all.items() if k in ()}
    del _L0_xattn_all

    def _L0_attn_setup():
        import jax, jax.numpy as jnp
        import numpy as np
        D_MODEL = 1024
        NUM_HEADS = 16
        DK = D_MODEL // NUM_HEADS
        key = jax.random.key(seed)
        kx, kq, kk, kv, ko = jax.random.split(key, 5)
        s = 1.0 / np.sqrt(D_MODEL)
        return {'x': jax.random.normal(kx, (4, 1024, D_MODEL), dtype=jnp.float32), 'Wq': jax.random.normal(kq, (D_MODEL, D_MODEL), dtype=jnp.float32) * s, 'Wk': jax.random.normal(kk, (D_MODEL, D_MODEL), dtype=jnp.float32) * s, 'Wv': jax.random.normal(kv, (D_MODEL, D_MODEL), dtype=jnp.float32) * s, 'Wo': jax.random.normal(ko, (D_MODEL, D_MODEL), dtype=jnp.float32) * s}
    _L0_attn_all = _L0_attn_setup()
    _L0_attn_in = {k: v for k, v in _L0_attn_all.items() if k in ('Wq', 'Wk', 'Wv', 'Wo')}
    del _L0_attn_all

    def _L0_ffn_setup():
        import jax, jax.numpy as jnp
        import numpy as np
        DIM_IN = 1024
        DIM_HIDDEN = 4096
        key = jax.random.key(seed)
        k_x, k_g, k_u, k_d = jax.random.split(key, 4)
        s_in = 1.0 / np.sqrt(DIM_IN)
        s_hid = 1.0 / np.sqrt(DIM_HIDDEN)
        x = jax.random.normal(k_x, (4, 1024, DIM_IN), dtype=jnp.float32)
        w_gate = jax.random.uniform(k_g, (DIM_HIDDEN, DIM_IN), jnp.float32, -s_in, s_in)
        w_up = jax.random.uniform(k_u, (DIM_HIDDEN, DIM_IN), jnp.float32, -s_in, s_in)
        w_down = jax.random.uniform(k_d, (DIM_IN, DIM_HIDDEN), jnp.float32, -s_hid, s_hid)
        return {'x': x, 'w_gate': w_gate, 'w_up': w_up, 'w_down': w_down}
    _L0_ffn_all = _L0_ffn_setup()
    _L0_ffn_in = {k: v for k, v in _L0_ffn_all.items() if k in ('w_gate', 'w_up', 'w_down')}
    del _L0_ffn_all
    return {'x': x, 'ctx_2048': ctx_2048, 'mask_BxS2_bk0': mask_BxS2_bk0, 'L0_attn_Wq': _L0_attn_in['Wq'], 'L0_attn_Wk': _L0_attn_in['Wk'], 'L0_attn_Wv': _L0_attn_in['Wv'], 'L0_attn_Wo': _L0_attn_in['Wo'], 'L0_ffn_w_gate': _L0_ffn_in['w_gate'], 'L0_ffn_w_up': _L0_ffn_in['w_up'], 'L0_ffn_w_down': _L0_ffn_in['w_down']}

def reference(x, ctx_2048, mask_BxS2_bk0, L0_attn_Wq, L0_attn_Wk, L0_attn_Wv, L0_attn_Wo, L0_ffn_w_gate, L0_ffn_w_up, L0_ffn_w_down):
    import jax
    import jax.numpy as jnp

    def _L0_xattn_ref(hidden_states, memory_tokens, memory_mask):
        import jax, jax.numpy as jnp
        import numpy as np
        B, S, D = hidden_states.shape
        scale = 1.0 / jnp.sqrt(jnp.asarray(D, hidden_states.dtype))
        scores = jnp.einsum('bsd,bmd->bsm', hidden_states, memory_tokens) * scale
        neg_inf = jnp.asarray(-1e+30, scores.dtype)
        scores = jnp.where(memory_mask[:, None, :], scores, neg_inf)
        attn = jax.nn.softmax(scores, axis=-1)
        readout = jnp.einsum('bsm,bmd->bsd', attn, memory_tokens)
        valid_b = jnp.any(memory_mask, axis=-1)
        out = jnp.where(valid_b[:, None, None], readout, jnp.zeros_like(readout))
        return out

    def _L0_attn_ref(x, Wq, Wk, Wv, Wo):
        import jax, jax.numpy as jnp
        import numpy as np
        D_MODEL = 1024
        NUM_HEADS = 16
        DK = D_MODEL // NUM_HEADS
        B, S, D = x.shape
        H, dk = (NUM_HEADS, DK)
        q = (x @ Wq.T).reshape(B, S, H, dk).transpose(0, 2, 1, 3)
        k = (x @ Wk.T).reshape(B, S, H, dk).transpose(0, 2, 1, 3)
        v = (x @ Wv.T).reshape(B, S, H, dk).transpose(0, 2, 1, 3)
        scores = jnp.einsum('bhqd,bhkd->bhqk', q, k) / jnp.sqrt(jnp.float32(dk))
        causal = jnp.tril(jnp.ones((S, S), dtype=bool))
        scores = jnp.where(causal, scores, jnp.finfo(scores.dtype).min)
        probs = jax.nn.softmax(scores, axis=-1)
        attn = jnp.einsum('bhqk,bhkd->bhqd', probs, v)
        attn = attn.transpose(0, 2, 1, 3).reshape(B, S, D)
        return attn @ Wo.T

    def _L0_ffn_ref(x, w_gate, w_up, w_down):
        import jax, jax.numpy as jnp
        import numpy as np
        DIM_IN = 1024
        DIM_HIDDEN = 4096
        gate = jnp.einsum('bsd,hd->bsh', x, w_gate)
        up = jnp.einsum('bsd,hd->bsh', x, w_up)
        gated = jax.nn.silu(gate) * up
        return jnp.einsum('bsh,dh->bsd', gated, w_down)
    x = x + _L0_xattn_ref(_layernorm(x, axis=-1), ctx_2048, mask_BxS2_bk0)
    x = x + _L0_attn_ref(_layernorm(x, axis=-1), L0_attn_Wq, L0_attn_Wk, L0_attn_Wv, L0_attn_Wo)
    x = x + _L0_ffn_ref(_layernorm(x, axis=-1), L0_ffn_w_gate, L0_ffn_w_up, L0_ffn_w_down)
    return x

_drawn_inputs = setup_inputs


def setup_inputs(seed=0):
    import zlib

    import numpy as np

    out = dict(_drawn_inputs(seed))
    spreads = {}
    factors = {}
    for name, (base, spread) in spreads.items():
        noise = np.random.default_rng([zlib.crc32(name.encode()), seed]).standard_normal(out[name].shape)
        drawn = base * np.exp(spread * noise) if base else spread * noise
        out[name] = jnp.asarray(drawn.astype(out[name].dtype))
    for name, factor in factors.items():
        out[name] = (out[name] * factor).astype(out[name].dtype)
    return out
```

```python
from contextlib import ExitStack

import concourse.bass as bass
from concourse import mybir

ALU = mybir.AluOpType
ACT = mybir.ActivationFunctionType
AX = mybir.AxisListType
F32 = mybir.dt.float32
F32R = mybir.dt.float32r
U8 = mybir.dt.uint8

P = 128
B, S, D, M = 32, 32, 1024, 257
MB = M // P * P
MT = MB // P
NT = B * S // P
BT = P // S
KD = D // P
HALF = 512
UNIT = 2048
H, DK = 16, 64
HG = 4
NG = H // HG
FT = HG * DK // P
DH = 4096
NC = DH // 256
SLOTS = 4
MC = MB + B
PTW = MB + S
BIG = 1e30
CAUSAL_FILL = -3e38
EPS = 1e-5
CTX_UNITS = 2 * B
ATT_PAIRS = 4 * NG
CTX_USES = CTX_UNITS // SLOTS
ATT_USES = CTX_USES + ATT_PAIRS // SLOTS
FFN_SLOTS = 3


def build(nc, x_in, ctx_in, w_in, mask_in, ext_in, ext_t_in, out):
    stack = ExitStack()
    with stack:
        def sb(where, name, shape, dt=F32):
            return where.enter_context(nc.sbuf_tensor(name, shape, dt))

        def sem(name):
            return stack.enter_context(nc.semaphore(name))

        x = sb(stack, "x", [P, NT, D])
        raw = [sb(stack, f"raw{i}", [P, UNIT]) for i in range(SLOTS)]
        xn = [sb(stack, f"xn{i}", [P, D]) for i in range(2)]
        ident = sb(stack, "ident", [P, P])
        causal = sb(stack, "causal", [P, S])
        stats = sb(stack, "stats", [P, NT, 2, 6])
        mv = sb(stack, "mv", [P, NT, 2])
        std = sb(stack, "std", [P, NT])
        rstd = sb(stack, "rstd", [P, NT, 1])

        a = ExitStack()
        cT_hi = [sb(a, f"cT_hi{i}", [P, 2, KD, MB], F32R) for i in range(2)]
        cT_lo = [sb(a, f"cT_lo{i}", [P, 2, KD, MB], F32R) for i in range(2)]
        cN_hi = [sb(a, f"cN_hi{i}", [P, MT, D], F32R) for i in range(2)]
        cN_lo = [sb(a, f"cN_lo{i}", [P, MT, D], F32R) for i in range(2)]
        xt_hi = sb(a, "xt_hi", [P, KD, P], F32R)
        xt_lo = sb(a, "xt_lo", [P, KD, P], F32R)
        pz_hi = sb(a, "pz_hi", [P, BT * PTW], F32R)
        pz_lo = sb(a, "pz_lo", [P, BT * PTW], F32R)
        pe_hi = sb(a, "pe_hi", [B, P], F32R)
        pe_lo = sb(a, "pe_lo", [B, P], F32R)
        ext_hi = sb(a, "ext_hi", [B, D], F32R)
        ext_lo = sb(a, "ext_lo", [B, D], F32R)
        extT_hi = sb(a, "extT_hi", [P, KD, B], F32R)
        extT_lo = sb(a, "extT_lo", [P, KD, B], F32R)
        mask = sb(a, "mask", [P, NT, MC], U8)
        valid = sb(a, "valid", [P, NT, 1])
        fill = sb(a, "fill", [P, MC])
        sc_sb = sb(a, "sc_sb", [P, MC])
        prob = sb(a, "prob", [P, MC])
        neg_top = sb(a, "neg_top", [P, 1])
        total = sb(a, "total", [P, 1])
        inv = sb(a, "inv", [P, 1])
        inv_valid = sb(a, "inv_valid", [P, 1])
        a.close()

        w_hi = [sb(stack, f"w_hi{i}", [P, UNIT], F32R) for i in range(2)]
        w_lo = [sb(stack, f"w_lo{i}", [P, UNIT], F32R) for i in range(2)]
        xT_hi = sb(stack, "xT_hi", [P, KD, NT * P], F32R)
        xT_lo = sb(stack, "xT_lo", [P, KD, NT * P], F32R)
        s = ExitStack()
        qT = sb(s, "qT", [P, FT, NT * P])
        kT = sb(s, "kT", [P, FT, NT * P])
        v = sb(s, "v", [P, NT, HG * DK])
        att = [sb(s, f"att{i}", [P, 2, 2, S]) for i in range(2)]
        att_p = [sb(s, f"att_p{i}", [P, HG, S]) for i in range(2)]
        att_z = [sb(s, f"att_z{i}", [P, HG, P]) for i in range(2)]
        att_top = sb(s, "att_top", [P, HG])
        att_sum = sb(s, "att_sum", [P, HG])
        att_inv = [sb(s, f"att_inv{i}", [P, HG]) for i in range(2)]
        o_sb = sb(s, "o_sb", [P, HG * DK])
        oT_hi = sb(s, "oT_hi", [P, FT, P], F32R)
        oT_lo = sb(s, "oT_lo", [P, FT, P], F32R)
        s.close()
        w_hi.append(sb(stack, "w_hi2", [P, UNIT], F32R))
        w_lo.append(sb(stack, "w_lo2", [P, UNIT], F32R))
        h_hi = sb(stack, "h_hi", [P, 2, NT * P], F32R)
        h_lo = sb(stack, "h_lo", [P, 2, NT * P], F32R)

        ps = stack.enter_context(nc.psum_tensor("ps", [P, 8, HALF], F32))

        x_full = [sem(f"x_full{i}") for i in range(2)]
        small_full = [sem(f"small_full{i}") for i in range(3)]
        stored = sem("stored")
        raw_full = [sem(f"raw_full{i}") for i in range(SLOTS)]
        split_done = [sem(f"split_done{i}") for i in range(SLOTS)]
        hi_done = sem("hi_done")
        const_done = sem("const_done")
        dve_own = sem("dve_own")
        ext_hi_done = sem("ext_hi_done")
        ext_done = sem("ext_done")
        var_ready = sem("var_ready")
        std_ready = sem("std_ready")
        xn_ready = sem("xn_ready")
        xt_psum = sem("xt_psum")
        xt_hi_done = sem("xt_hi_done")
        xt_ready = sem("xt_ready")
        scores_done = sem("scores_done")
        scores_read = sem("scores_read")
        top_ready = sem("top_ready")
        exp_done = sem("exp_done")
        pt_psum = sem("pt_psum")
        pt_hi_done = sem("pt_hi_done")
        pt_ready = sem("pt_ready")
        ctx_used = sem("ctx_used")
        readout_done = sem("readout_done")
        readout_free = sem("readout_free")
        q_done = sem("q_done")
        k_done = sem("k_done")
        v_done = sem("v_done")
        q_kept = sem("q_kept")
        k_kept = sem("k_kept")
        v_kept = sem("v_kept")
        att_done = sem("att_done")
        att_read = sem("att_read")
        att_shifted = sem("att_shifted")
        att_exp = sem("att_exp")
        att_turned = sem("att_turned")
        z_zero = sem("z_zero")
        pv_done = sem("pv_done")
        o_ready = sem("o_ready")
        oT_psum = sem("oT_psum")
        oT_hi_done = sem("oT_hi_done")
        oT_ready = sem("oT_ready")
        wo_done = sem("wo_done")
        wo_free = sem("wo_free")
        gu_done = sem("gu_done")
        silu_done = sem("silu_done")
        h_done = sem("h_done")
        h_hi_done = sem("h_hi_done")
        h_ready = sem("h_ready")
        down_done = sem("down_done")
        down_added = sem("down_added")

        def sg(half):
            return xn[0][:, half * HALF:(half + 1) * HALF]

        def gf(half):
            return xn[1][:, half * HALF:(half + 1) * HALF]

        block = stack.enter_context(nc.Block())

        def turned_unit(t, b):
            return b, (0 if isinstance(t, int) and t == 0 else t * 2 - 1)

        def rows_unit(t, b, last=False):
            return b, (CTX_USES - 1 if last else t * 2 + 2)

        @block.sync
        def _(sync):
            for i in range(2):
                sync.dma_start(x[:, i * NT // 2:(i + 1) * NT // 2, :],
                               x_in[:, i * NT // 2:(i + 1) * NT // 2, :]).then_inc(x_full[i], 16)
            for i in range(SLOTS):
                sync.dma_start(raw[i][:, :], ctx_in[i]).then_inc(raw_full[i], 16)
            with sync.Fori(1, CTX_USES) as u:
                for i in range(SLOTS):
                    sync.wait_ge(split_done[i], u)
                    sync.dma_start(raw[i][:, :], ctx_in[u * SLOTS + i]).then_inc(raw_full[i], 16)
            with sync.Fori(0, NG) as g:
                for i in range(SLOTS):
                    sync.wait_ge(split_done[i], g + CTX_USES)
                    sync.dma_start(raw[i][:, :], w_in[g * SLOTS + i]).then_inc(raw_full[i], 16)
            with sync.Fori(0, NC) as c:
                for i in range(FFN_SLOTS):
                    sync.wait_ge(split_done[i], c + ATT_USES)
                    sync.dma_start(raw[i][:, :], w_in[c * FFN_SLOTS + (ATT_PAIRS + i)])\
                        .then_inc(raw_full[i], 16)
            for t in range(NT):
                sync.wait_ge(down_added, 2 * NT * (NC - 1) + 2 * t + 2)
                sync.dma_start(out[t * P:(t + 1) * P, :], x[:, t, :]).then_inc(stored, 16)
            sync.wait_ge(stored, 16 * NT)

        @block.gpsimd
        def _(pool):
            pool.dma_start(mask[:, :, :], mask_in).then_inc(small_full[0], 16)
            pool.memset(ident[:, :], 0.0).then_inc(const_done, 1)
            pool.memset(causal[:, :], 0.0).then_inc(const_done, 1)
            pool.memset(pz_hi[:, :].bitcast(F32), 0.0).then_inc(const_done, 1)
            pool.memset(pz_lo[:, :].bitcast(F32), 0.0).then_inc(const_done, 1)
            pool.wait_ge(const_done, 4)
            pool.affine_select(out=ident[:, :], in_=ident[:, :], compare_op=ALU.not_equal, fill=1.0,
                               base=0, pattern=[[-1, P]], channel_multiplier=1).then_inc(const_done, 1)
            for b in range(BT):
                q = slice(b * S, (b + 1) * S)
                pool.wait_ge(const_done, 5 + b)
                pool.affine_select(out=causal[q, :], in_=causal[q, :], compare_op=ALU.is_ge,
                                   fill=CAUSAL_FILL, base=0, pattern=[[-1, S]],
                                   channel_multiplier=1).then_inc(const_done, 1)

            def lo(slot, use, unit, dst, hi):
                pool.wait_ge(hi_done, unit + 1)
                pool.tensor_tensor(dst, raw[slot][:, :], hi.bitcast(F32), ALU.subtract)\
                    .then_inc(split_done[slot], 1)

            def turned(t, unit):
                lo(3, None, unit, flat(cT_lo[1][:, 1]), flat(cT_hi[1][:, 1]))

            def rows(unit):
                lo(3, None, unit, flat(cN_lo[1][:, :, :]), flat(cN_hi[1][:, :, :]))

            pool.wait_ge(const_done, 5 + BT)
            turned(0, 3)
            turned(1, 7)
            with pool.Fori(1, NT - 1) as t:
                rows(t * 8 + 3)
                turned(t + 1, t * 8 + 7)
            rows(CTX_UNITS - 5)
            rows(CTX_UNITS - 1)

            def weights(slot, use, pair, wslot):
                pool.wait_ge(hi_done, pair + (CTX_UNITS + 1))
                pool.tensor_tensor(w_lo[wslot][:, :], raw[slot][:, :], w_hi[wslot][:, :].bitcast(F32),
                                   ALU.subtract).then_inc(split_done[slot], 1)

            weights(0, None, 0, 0)
            pool.wait_ge(wo_free, 1)
            for i in range(2):
                pool.memset(att_z[i][:, :, :], 0.0).then_inc(z_zero, 1)
            with pool.Fori(0, NG - 1) as g:
                for i in range(SLOTS):
                    weights((i + 1) % SLOTS, None, g * SLOTS + (i + 1), (i + 1) % 2)
            for i in range(SLOTS):
                weights((i + 1) % SLOTS, None, (NG - 1) * SLOTS + i + 1, (i + 1) % 2)
            with pool.Fori(0, NC - 1) as c:
                for i in range(FFN_SLOTS):
                    k = (i + 1) % FFN_SLOTS
                    weights(k, None, c * FFN_SLOTS + (ATT_PAIRS + i + 1), k)
            for i in (1, 2):
                weights(i, None, (NC - 1) * FFN_SLOTS + ATT_PAIRS + i, i)

        @block.scalar
        def _(act):
            act.dma_start(xn[1][0:B, :], ext_in).then_inc(small_full[1], 16)
            act.dma_start(prob[:, 0:KD * B], ext_t_in).then_inc(small_full[2], 16)

            def hi(slot, use, dst):
                act.wait_ge(raw_full[slot], (use + 1) * 16)
                act.activation(dst, raw[slot][:, :], ACT.Copy).then_inc(hi_done, 1)

            def turned(t, b):
                slot, use = turned_unit(t, b)
                hi(slot, use, flat(cT_hi[b // 2][:, b % 2]))

            def rows(t, b, last=False):
                slot, use = rows_unit(t, b, last)
                hi(slot, use, flat(cN_hi[b % 2][:, :, :]))

            act.wait_ge(small_full[1], 16)
            act.activation(ext_hi[:, :], xn[1][0:B, :], ACT.Copy).then_inc(ext_hi_done, 1)
            act.wait_ge(small_full[2], 16)
            act.activation(flat(extT_hi[:, :, :]), prob[:, 0:KD * B], ACT.Copy).then_inc(ext_hi_done, 1)

            def root(n):
                act.wait_ge(var_ready, n)
                act.activation(std[:, :], std[:, :], ACT.Sqrt).then_inc(std_ready, 1)

            root(1)
            for b in range(BT):
                turned(0, b)

            def tile(t, first=False, last=False):
                act.wait_ge(xt_psum, t + 1)
                act.activation(flat(xt_hi[:, :, :]), flat(ps[:, 3:5, :]), ACT.Copy).then_inc(xt_hi_done, 1)
                if not first:
                    for b in (2, 3):
                        act.wait_ge(ctx_used, t * 4 + (b - 5))
                        rows(t - 1, b)
                if not last:
                    act.wait_ge(scores_done, t * 2 + 1)
                    turned(t + 1, 0)
                    turned(t + 1, 1)
                act.wait_ge(top_ready, t + 1)
                act.activation(prob[:, :], sc_sb[:, :], ACT.Exp, bias=neg_top[:, 0:1],
                               accum_out=total[:, 0:1]).then_inc(exp_done, 1)
                if not last:
                    act.wait_ge(scores_done, t * 2 + 2)
                    turned(t + 1, 2)
                    turned(t + 1, 3)
                act.wait_ge(pt_psum, t + 1)
                if first:
                    act.wait_ge(const_done, 4)
                act.activation(blocks(pz_hi), turned_psum(ps), ACT.Copy)
                act.activation(pe_hi[:, :], ps[0:B, 5, MB:MB + P], ACT.Copy).then_inc(pt_hi_done, 1)
                for b in (0, 1):
                    if not first:
                        act.wait_ge(ctx_used, t * 4 + (b - 1))
                    rows(t, b, last)

            tile(0, first=True)
            with act.Fori(1, NT - 1) as t:
                tile(t)
            tile(NT - 1, last=True)
            for b in (2, 3):
                act.wait_ge(ctx_used, 4 * (NT - 1) + b - 1)
                rows(NT - 1, b, True)

            def weights(slot, use, wslot):
                act.wait_ge(raw_full[slot], (use + 1) * 16)
                act.activation(w_hi[wslot][:, :], raw[slot][:, :], ACT.Copy).then_inc(hi_done, 1)

            act.wait_ge(scores_done, 2 * NT)
            weights(0, CTX_USES, 0)

            def norm(n):
                root(n + 1)
                for t in range(NT):
                    act.wait_ge(xt_psum, n * NT + t + 1)
                    act.activation(xT_hi[:, :, t * P:(t + 1) * P], tile_psum(ps, t), ACT.Copy)\
                        .then_inc(xt_hi_done, 1)

            norm(1)

            def group(g, last=False):
                for k in range(4):
                    if k == 0:
                        act.wait_ge(wo_free, g * 8 + 1)
                    else:
                        act.wait_ge((q_done, k_done, v_done)[k - 1], (g + 1) * (4, 4, 8)[k - 1])
                    weights((k + 1) % 4, g + (CTX_USES + (k + 1) // 4), (k + 1) % 2)
                    if k == 0:
                        for j in range(2 * FT):
                            act.wait_ge(q_done, g * 4 + (j + 1))
                            act.activation(qT[:, j // 2, (j % 2) * HALF:(j % 2 + 1) * HALF],
                                           ps[:, j, :], ACT.Copy, scale=DK ** -0.5).then_inc(q_kept, 1)
                    if k == 2:
                        for t in range(NT):
                            act.wait_ge(v_done, g * 8 + (t + 1))
                            act.activation(v[:, t, :], ps[:, t, 0:HG * DK], ACT.Copy).then_inc(v_kept, 1)
                for st in range(NT + 2):
                    if st >= 2:
                        act.wait_ge(oT_psum, g * 8 + (st - 1))
                        act.activation(flat(oT_hi[:, :, :]), ps[:, 5, 0:FT * P], ACT.Copy)\
                            .then_inc(oT_hi_done, 1)
                    if st < NT:
                        act.wait_ge(att_shifted, g * 8 + (st + 1))
                        act.activation(flat(att_p[st % 2][:, :, :]), flat3(att[st % 2]), ACT.Exp)\
                            .then_inc(att_exp, 1)

            with act.Fori(0, NG - 1) as g:
                group(g)
            group(NG - 1, True)
            act.wait_ge(wo_done, NG * NT)
            weights(1, ATT_USES, 1)
            norm(2)

            def chunk(c, first=False, last=False):
                for k in range(3):
                    if not (first and k == 0) and not (last and k == 2):
                        if k == 0:
                            act.wait_ge(gu_done, c * 4)
                        elif k == 2:
                            act.wait_ge(gu_done, c * 4 + 2)
                        elif not first:
                            act.wait_ge(down_done, c * 16)
                        nxt = (k + 1) % 3
                        weights(nxt, c + (ATT_USES + (k + 1) // 3), nxt)
                    if k < 2:
                        for half in range(2):
                            n = 2 * k + half
                            act.wait_ge(gu_done, c * 4 + (n + 1))
                            act.activation(sg(half), ps[:, 2 * n, :], ACT.Silu).then_inc(silu_done, 1)
                            act.wait_ge(h_done, c * 4 + (n + 1))
                            act.activation(h_hi[:, k, half * HALF:(half + 1) * HALF], gf(half), ACT.Copy)\
                                .then_inc(h_hi_done, 1)

            chunk(0, first=True)
            with act.Fori(1, NC - 1) as c:
                chunk(c)
            chunk(NC - 1, last=True)

        @block.tensor
        def _(pe):
            def three(dst, stat, moving, start, stop):
                pe.matmul(dst, stat[0], moving[0], start=start, stop=False)
                pe.matmul(dst, stat[0], moving[1], start=False, stop=False)
                return pe.matmul(dst, stat[1], moving[0], start=False, stop=stop)

            def unit_ready(slot_use):
                slot, use = slot_use
                pe.wait_ge(split_done[slot], use + 1)

            def turn(src, banks):
                for k in range(KD):
                    mm = pe.transpose(ps[:, banks + k // 4, (k % 4) * P:(k % 4 + 1) * P],
                                      src[:, k * P:(k + 1) * P], ident[:, :])
                mm.then_inc(xt_psum, 1)

            def readout(t, batches, last=False):
                for b in batches:
                    unit_ready(rows_unit(t, b, last))
                    for half in range(2):
                        for m in range(MT):
                            col = b * MB + m * P
                            mm = three(ps[:, 6 + half, :],
                                       (pz_hi[:, col:col + P], pz_lo[:, col:col + P]),
                                       (cN_hi[b % 2][:, m, half * HALF:(half + 1) * HALF],
                                        cN_lo[b % 2][:, m, half * HALF:(half + 1) * HALF]),
                                       start=(b == 0 and m == 0), stop=False)
                    mm.then_inc(ctx_used, 1)
                if 3 in batches:
                    for half in range(2):
                        mm = three(ps[:, 6 + half, :], (pe_hi[:, :], pe_lo[:, :]),
                                   (ext_hi[:, half * HALF:(half + 1) * HALF],
                                    ext_lo[:, half * HALF:(half + 1) * HALF]), start=False, stop=True)
                    mm.then_inc(readout_done, 1)

            def tile(t, first=False):
                pe.wait_ge(xn_ready, t + 1)
                turn(xn[0], 3)
                if not first:
                    pe.wait_ge(pt_ready, t)
                    pe.wait_ge(readout_free, t)
                    readout(t - 1, (0, 1))
                pe.wait_ge(xt_ready, t + 1)
                if first:
                    pe.wait_ge(ext_done, 1)
                else:
                    pe.wait_ge(scores_read, t)
                for k in range(KD):
                    three(ps[:, 2, 0:B], (xt_hi[:, k, :], xt_lo[:, k, :]),
                          (extT_hi[:, k, :], extT_lo[:, k, :]), start=(k == 0), stop=(k == KD - 1))
                for pair in range(2):
                    for b in (2 * pair, 2 * pair + 1):
                        unit_ready(turned_unit(t, b))
                    for k in range(KD):
                        mm = three(ps[:, pair, :].rearrange("p (b m) -> p b m", b=2),
                                   (xt_hi[:, k, :], xt_lo[:, k, :]),
                                   (cT_hi[pair][:, :, k, :], cT_lo[pair][:, :, k, :]),
                                   start=(k == 0), stop=(k == KD - 1))
                    mm.then_inc(scores_done, 1)
                if not first:
                    readout(t - 1, (2, 3))
                pe.wait_ge(exp_done, t + 1)
                for m in range(MT):
                    pe.transpose(ps[:, 5, m * P:(m + 1) * P], prob[:, m * P:(m + 1) * P], ident[:, :])
                pe.transpose(ps[0:B, 5, MB:MB + P], prob[:, MB:MC], ident[:, :]).then_inc(pt_psum, 1)

            pe.wait_ge(const_done, 5)
            tile(0, first=True)
            with pe.Fori(1, NT) as t:
                tile(t)
            pe.wait_ge(pt_ready, NT)
            pe.wait_ge(readout_free, NT)
            readout(NT - 1, (0, 1, 2, 3), last=True)

            def norm(n):
                for t in range(NT):
                    pe.wait_ge(xn_ready, n * NT + t + 1)
                    if t >= 4:
                        pe.wait_ge(xt_ready, n * NT + t - 3)
                    turn(xn[t % 2], 2 * (t % 4))
                pe.wait_ge(xt_ready, n * NT + NT)

            norm(1)

            def stationary(slot, unit, k):
                at = (unit * KD + k) * P
                return w_hi[slot][:, at:at + P], w_lo[slot][:, at:at + P]

            def tokens(k, at, n):
                return xT_hi[:, k, at:at + n], xT_lo[:, k, at:at + n]

            def group(g):
                for kind, done in ((0, q_done), (1, k_done)):
                    pe.wait_ge(split_done[kind], g + (CTX_USES + 1))
                    for j in range(2 * FT):
                        if kind and j == 2:
                            pe.wait_ge(wo_free, g * 8 + 1)
                        for k in range(KD):
                            mm = three(ps[:, 4 * kind + j, :], stationary(kind, j // 2, k),
                                       tokens(k, (j % 2) * HALF, HALF), start=(k == 0), stop=(k == KD - 1))
                        mm.then_inc(done, 1)
                pe.wait_ge(split_done[2], g + (CTX_USES + 1))
                W = HG * DK
                for t in range(NT):
                    if t < 4:
                        pe.wait_ge(q_kept, g * 4 + (t + 1))
                    else:
                        pe.wait_ge(k_kept, g * 4 + (t - 3))
                    for k in range(KD):
                        mm = three(ps[:, t, 0:W], tokens(k, t * P, P),
                                   (w_hi[0][:, k * W:(k + 1) * W], w_lo[0][:, k * W:(k + 1) * W]),
                                   start=(k == 0), stop=(k == KD - 1))
                    mm.then_inc(v_done, 1)
                pe.wait_ge(v_kept, g * 8 + 8)
                for st in range(NT + 2):
                    if st >= 2:
                        pe.wait_ge(o_ready, g * 8 + (st - 1))
                        for f in range(FT):
                            mm = pe.transpose(ps[:, 5, f * P:(f + 1) * P], o_sb[:, f * P:(f + 1) * P],
                                              ident[:, :])
                        mm.then_inc(oT_psum, 1)
                    if st < NT:
                        if st >= 2:
                            pe.wait_ge(att_read, g * 8 + (st - 1))
                        for h in range(HG):
                            r = slice((h % 2) * DK, (h % 2 + 1) * DK)
                            mm = pe.matmul(ps[:, 2 * (st % 2) + h % 2, (h // 2) * P:(h // 2 + 1) * P],
                                           qT[r, h // 2, st * P:(st + 1) * P],
                                           kT[r, h // 2, st * P:(st + 1) * P], start=True, stop=True)
                        mm.then_inc(att_done, 1)
                    if 1 <= st <= NT:
                        pe.wait_ge(att_turned, g * 8 + st)
                        for h in range(HG):
                            mm = pe.matmul(ps[:, 4, h * DK:(h + 1) * DK], att_z[(st - 1) % 2][:, (h % 2) * 2 + h // 2, :],
                                           v[:, st - 1, h * DK:(h + 1) * DK], start=True, stop=True)
                        mm.then_inc(pv_done, 1)
                    if st >= 2:
                        if st == 2:
                            pe.wait_ge(split_done[3], g + (CTX_USES + 1))
                        pe.wait_ge(oT_ready, g * 8 + (st - 1))
                        pe.wait_ge(wo_free, g * 8 + (st - 1))
                        for f in range(FT):
                            for half in range(2):
                                at = f * D + half * HALF
                                mm = three(ps[:, 6 + half, :], (oT_hi[:, f, :], oT_lo[:, f, :]),
                                           (w_hi[1][:, at:at + HALF], w_lo[1][:, at:at + HALF]),
                                           start=(f == 0), stop=(f == FT - 1))
                        mm.then_inc(wo_done, 1)

            pe.wait_ge(z_zero, 2)
            with pe.Fori(0, NG) as g:
                group(g)
            pe.wait_ge(wo_free, NG * 8 + 1)
            norm(2)

            def chunk(c, first=False):
                for k in range(2):
                    pe.wait_ge(split_done[k], c + (ATT_USES + 1))
                    for half in range(2):
                        n = 2 * k + half
                        if not first:
                            pe.wait_ge(down_added, (c - 1) * 16 + (8 + 2 * n + 2))
                        for u in range(2):
                            for kk in range(KD):
                                mm = three(ps[:, 2 * n + u, :], stationary(k, u, kk),
                                           tokens(kk, half * HALF, HALF), start=(kk == 0),
                                           stop=(kk == KD - 1))
                        mm.then_inc(gu_done, 1)
                pe.wait_ge(split_done[2], c + (ATT_USES + 1))
                for i in range(2 * NT):
                    t, half = i // 2, i % 2
                    if i == 0:
                        pe.wait_ge(h_ready, c * 4 + 3)
                    if i == NT:
                        pe.wait_ge(h_ready, c * 4 + 4)
                    if i < 8:
                        pe.wait_ge(h_done, c * 4 + (i // 2 + 1))
                    else:
                        pe.wait_ge(down_added, c * 16 + (i - 7))
                    for k in range(2):
                        at = k * D + half * HALF
                        mm = three(ps[:, i % 8, :],
                                   (h_hi[:, k, t * P:(t + 1) * P], h_lo[:, k, t * P:(t + 1) * P]),
                                   (w_hi[2][:, at:at + HALF], w_lo[2][:, at:at + HALF]),
                                   start=(k == 0), stop=(k == 1))
                    mm.then_inc(down_done, 1)

            chunk(0, first=True)
            with pe.Fori(1, NC) as c:
                chunk(c)

        @block.vector
        def _(dve):
            own = [0, 0]

            class at:
                base = 0

            def mark(ins):
                own[0] += 1
                ins.then_inc(dve_own, 1)

            def settle():
                dve.wait_ge(dve_own, at.base + own[0])

            def lo(slot, unit, dst, hi):
                dve.wait_ge(hi_done, unit + 1)
                dve.tensor_tensor(dst, raw[slot][:, :], hi.bitcast(F32), ALU.subtract)\
                    .then_inc(split_done[slot], 1)

            def turned(t, b):
                unit = t * 8 + (b - 4) if not (isinstance(t, int) and t == 0) else b
                lo(b, unit, flat(cT_lo[b // 2][:, b % 2]), flat(cT_hi[b // 2][:, b % 2]))

            def rows(t, b, last=False):
                unit = CTX_UNITS - 4 + b if last else t * 8 + (8 + b)
                lo(b, unit, flat(cN_lo[b % 2][:, :, :]), flat(cN_hi[b % 2][:, :, :]))

            def tile_stats(t):
                for half in range(2):
                    ins = dve.bn_stats(stats[:, t, half, :], x[:, t, half * HALF:(half + 1) * HALF])
                mark(ins)

            def scales(n):
                settle()
                for t in range(NT):
                    ins = dve.bn_aggr(mv[:, t, :], stats[:, t, :, :])
                mark(ins)
                settle()
                dve.tensor_scalar(std[:, :], mv[:, :, 1], EPS, None, ALU.add).then_inc(var_ready, 1)
                dve.wait_ge(std_ready, n)
                mark(dve.reciprocal(rstd[:, :, 0], std[:, :]))
                settle()

            def normalise(t, dst):
                dve.tensor_scalar(dst, x[:, t, :], mv[:, t, 0:1], rstd[:, t, :],
                                  ALU.subtract, ALU.mult).then_inc(xn_ready, 1)

            dve.wait_ge(ext_hi_done, 2)
            dve.tensor_tensor(ext_lo[:, :], xn[1][0:B, :], ext_hi[:, :].bitcast(F32), ALU.subtract)
            dve.tensor_tensor(flat(extT_lo[:, :, :]), prob[:, 0:KD * B], flat(extT_hi[:, :, :]).bitcast(F32),
                              ALU.subtract).then_inc(ext_done, 1)
            dve.wait_ge(small_full[0], 16)
            mark(dve.tensor_reduce(valid[:, :, 0], mask[:, :, :], AX.X, ALU.max))
            for i in range(2):
                dve.wait_ge(x_full[i], 16)
                for t in range(i * NT // 2, (i + 1) * NT // 2):
                    tile_stats(t)
            scales(1)
            normalise(0, xn[0][:, :])
            for b in range(3):
                turned(0, b)

            def add_readout(t):
                dve.wait_ge(readout_done, t + 1)
                settle()
                for half in range(2):
                    part = x[:, t, half * HALF:(half + 1) * HALF]
                    ins = dve.scalar_tensor_tensor(out=part, in0=ps[:, 6 + half, :],
                                                   scalar=inv_valid[:, 0:1], in1=part,
                                                   op0=ALU.mult, op1=ALU.add)
                ins.then_inc(readout_free, 1)

            def tile(t, first=False, last=False):
                dve.wait_ge(xt_psum, t + 1)
                dve.wait_ge(xt_hi_done, t + 1)
                dve.tensor_tensor(flat(xt_lo[:, :, :]), flat(ps[:, 3:5, :]),
                                  flat(xt_hi[:, :, :]).bitcast(F32), ALU.subtract).then_inc(xt_ready, 1)
                if not last:
                    normalise(t + 1, xn[0][:, :])
                if first:
                    mark(dve.memset(inv_valid[:, :], 0.0))
                    settle()
                    dve.memset(inv_valid[:, :], 0.0).then_inc(readout_free, 1)
                mark(dve.tensor_scalar(fill[:, :], mask[:, t, :], BIG, -BIG, ALU.mult, ALU.add))
                if not first:
                    rows(t - 1, 2)
                if not last:
                    turned(t + 1, 0)
                    turned(t + 1, 1)
                dve.wait_ge(scores_done, t * 2 + 2)
                if not first:
                    dve.wait_ge(exp_done, t)
                for b in range(BT):
                    q = slice(b * S, (b + 1) * S)
                    dve.scalar_tensor_tensor(out=sc_sb[q, 0:MB],
                                             in0=ps[q, b // 2, (b % 2) * MB:(b % 2 + 1) * MB],
                                             scalar=D ** -0.5, in1=mask[q, t, 0:MB],
                                             op0=ALU.mult, op1=ALU.mult)
                ins = dve.scalar_tensor_tensor(out=sc_sb[:, MB:MC], in0=ps[:, 2, 0:B], scalar=D ** -0.5,
                                               in1=mask[:, t, MB:MC], op0=ALU.mult, op1=ALU.mult)
                ins.then_inc(scores_read, 1)
                dve.wait_ge(scores_read, t + 1)
                settle()
                mark(dve.tensor_tensor(sc_sb[:, :], sc_sb[:, :], fill[:, :], ALU.add))
                settle()
                dve.tensor_reduce(neg_top[:, :], sc_sb[:, :], AX.X, ALU.max, negate=True)\
                    .then_inc(top_ready, 1)
                if not last:
                    turned(t + 1, 2)
                if not first:
                    add_readout(t - 1)
                    dve.wait_ge(readout_free, t + 1)
                    tile_stats(t - 1)
                dve.wait_ge(exp_done, t + 1)
                mark(dve.reciprocal(inv[:, :], total[:, :]))
                settle()
                mark(dve.tensor_scalar(inv_valid[:, :], inv[:, :], valid[:, t, :], None, ALU.mult))
                dve.wait_ge(pt_hi_done, t + 1)
                if first:
                    dve.wait_ge(const_done, 4)
                dve.tensor_tensor(blocks(pz_lo), turned_psum(ps), blocks(pz_hi).bitcast(F32), ALU.subtract)
                dve.tensor_tensor(pe_lo[:, :], ps[0:B, 5, MB:MB + P], pe_hi[:, :].bitcast(F32),
                                  ALU.subtract).then_inc(pt_ready, 1)
                for b in (0, 1):
                    rows(t, b, last)

            tile(0, first=True)
            start = own[0]
            with dve.Fori(1, NT - 1) as t:
                at.base = (t - 1) * TILE_MARKS
                tile(t)
                assert own[0] - start == TILE_MARKS, own[0] - start
            at.base = TILE_MARKS * (NT - 3)
            tile(NT - 1, last=True)
            rows(NT - 1, 2, True)
            add_readout(NT - 1)
            dve.wait_ge(readout_free, NT + 1)
            tile_stats(NT - 1)

            def norm(n):
                scales(n + 1)
                for t in range(NT):
                    if t >= 2:
                        dve.wait_ge(xt_psum, n * NT + t - 1)
                    normalise(t, xn[t % 2][:, :])
                    if t >= 1:
                        turned_lo(n, t - 1)
                turned_lo(n, NT - 1)

            def turned_lo(n, t):
                dve.wait_ge(xt_hi_done, n * NT + t + 1)
                dve.tensor_tensor(xT_lo[:, :, t * P:(t + 1) * P], tile_psum(ps, t),
                                  xT_hi[:, :, t * P:(t + 1) * P].bitcast(F32), ALU.subtract)\
                    .then_inc(xt_ready, 1)

            norm(1)
            mark(dve.memset(att_top[:, :], 0.0))
            settle()
            dve.memset(att_top[:, :], 0.0).then_inc(wo_free, 1)

            def group(g, last=False):
                for j in range(2 * FT):
                    dve.wait_ge(k_done, g * 4 + (j + 1))
                    dve.tensor_copy(kT[:, j // 2, (j % 2) * HALF:(j % 2 + 1) * HALF], ps[:, 4 + j, :])\
                        .then_inc(k_kept, 1)
                for st in range(NT + 2):
                    two = st % 2
                    if st >= 2:
                        dve.wait_ge(oT_hi_done, g * 8 + (st - 1))
                        dve.tensor_tensor(flat(oT_lo[:, :, :]), ps[:, 5, 0:FT * P],
                                          flat(oT_hi[:, :, :]).bitcast(F32), ALU.subtract)\
                            .then_inc(oT_ready, 1)
                    if st < NT:
                        dve.wait_ge(att_done, g * 8 + (st + 1))
                        for b in range(BT):
                            q = slice(b * S, (b + 1) * S)
                            src = ps[q, 2 * two:2 * two + 2, 0:2 * P].rearrange("p e (h k) -> p e h k", h=2)
                            ins = dve.tensor_tensor(
                                att[two][q, :, :, :], src[:, :, :, b * S:(b + 1) * S],
                                causal[q, :].unsqueeze(1).unsqueeze(1).broadcast_to([S, 2, 2, S]), ALU.add)
                        ins.then_inc(att_read, 1)
                        dve.wait_ge(att_read, g * 8 + (st + 1))
                        rowsof = flat3(att[two]).rearrange("p (h k) -> p h k", h=HG)
                        mark(dve.tensor_reduce(att_top[:, :], rowsof, AX.X, ALU.max))
                        settle()
                        dve.tensor_tensor(rowsof, rowsof,
                                          att_top[:, :].unsqueeze(2).broadcast_to([P, HG, S]),
                                          ALU.subtract).then_inc(att_shifted, 1)
                    if 1 <= st <= NT:
                        dve.wait_ge(pv_done, g * 8 + st)
                        by = att_inv[(st - 1) % 2][:, :].rearrange("p (e h) -> p h e", e=2)
                        dve.tensor_tensor(o_sb[:, :].rearrange("p (h e d) -> p h e d", h=2, e=2),
                                          ps[:, 4, 0:HG * DK].rearrange("p (h e d) -> p h e d", h=2, e=2),
                                          by.unsqueeze(3).broadcast_to([P, 2, 2, DK]), ALU.mult)\
                            .then_inc(o_ready, 1)
                    if st < NT:
                        dve.wait_ge(att_exp, g * 8 + (st + 1))
                        for b in range(BT):
                            q = slice(b * S, (b + 1) * S)
                            ins = dve.transpose(att_z[two][q, :, b * S:(b + 1) * S], att_p[two][q, :, :])
                        ins.then_inc(att_turned, 1)
                        mark(dve.tensor_reduce(att_sum[:, :], att_p[two][:, :, :], AX.X, ALU.add))
                        settle()
                        mark(dve.reciprocal(att_inv[two][:, :], att_sum[:, :]))
                        settle()
                    if st >= 2:
                        dve.wait_ge(wo_done, g * 8 + (st - 1))
                        dve.wait_ge(wo_free, g * 8 + (st - 1))
                        for half in range(2):
                            part = x[:, st - 2, half * HALF:(half + 1) * HALF]
                            ins = dve.tensor_tensor(part, ps[:, 6 + half, :], part, ALU.add)
                        ins.then_inc(wo_free, 1)
                        if last:
                            dve.wait_ge(wo_free, g * 8 + st)
                            tile_stats(st - 2)

            dve.wait_ge(z_zero, 2)
            dve.wait_ge(const_done, 5 + BT)
            start = own[0]
            base = at.base
            with dve.Fori(0, NG - 1) as g:
                at.base = g * GROUP_MARKS + base
                group(g)
                assert own[0] - start == GROUP_MARKS, own[0] - start
            at.base = base + GROUP_MARKS * (NG - 2)
            group(NG - 1, True)
            norm(2)

            def chunk(c, first=False):
                for k in range(2):
                    for half in range(2):
                        n = 2 * k + half
                        cols = slice(half * HALF, (half + 1) * HALF)
                        dve.wait_ge(silu_done, c * 4 + (n + 1))
                        dve.tensor_tensor(gf(half), sg(half), ps[:, 2 * n + 1, :], ALU.mult)\
                            .then_inc(h_done, 1)
                        dve.wait_ge(h_hi_done, c * 4 + (n + 1))
                        dve.tensor_tensor(h_lo[:, k, cols], gf(half), h_hi[:, k, cols].bitcast(F32),
                                          ALU.subtract).then_inc(h_ready, 1)
                for i in range(2 * NT):
                    t, half = i // 2, i % 2
                    part = x[:, t, half * HALF:(half + 1) * HALF]
                    dve.wait_ge(down_done, c * 16 + (i + 1))
                    if not first:
                        dve.wait_ge(down_added, (c - 1) * 16 + (i + 1))
                    dve.tensor_tensor(part, ps[:, i % 8, :], part, ALU.add).then_inc(down_added, 1)

            chunk(0, first=True)
            with dve.Fori(1, NC) as c:
                chunk(c)


TILE_MARKS = 5
GROUP_MARKS = 24


def flat(ap):
    n = len(ap.shape)
    names = "abcd"[:n - 1]
    return ap if n == 2 else ap.rearrange(f"p {' '.join(names)} -> p ({' '.join(names)})")


def flat3(t):
    return t[:, :, :, :].rearrange("p a b c -> p (a b c)")


def tile_psum(ps, t):
    return ps[:, 2 * (t % 4):2 * (t % 4) + 2, :].rearrange("p e (k n) -> p (e k) n", n=P)


def blocks(padded):
    return padded[:, :].rearrange("p (b r) -> p b r", b=BT)[:, :, 0:MB]\
        .rearrange("p b (m n) -> p b m n", n=P)[:, :, :, 0:S]


def turned_psum(ps):
    return ps[:, 5, 0:MB].rearrange("p (m b n) -> p b m n", m=MT, b=BT)


def kernel(x, ctx_2048, mask_BxS2_bk0, L0_attn_Wq, L0_attn_Wk, L0_attn_Wv, L0_attn_Wo,
           L0_ffn_w_gate, L0_ffn_w_up, L0_ffn_w_down):
    import numpy as np
    import concourse.bacc as bacc
    from concourse.bass_utils import run_bass_kernel_spmd

    ctx, msk = np.asarray(ctx_2048), np.asarray(mask_BxS2_bk0)

    rows = ctx[:, :MB].reshape(B, MT, P, D).transpose(0, 2, 1, 3).reshape(B, P, UNIT)
    turned = ctx[:, :MB].transpose(0, 2, 1).reshape(B, KD, P, MB).transpose(0, 2, 1, 3).reshape(B, P, UNIT)
    order = [turned[b] for b in range(BT)]
    for t in range(NT):
        if t:
            order += [rows[(t - 1) * BT + b] for b in (2, 3)]
        if t + 1 < NT:
            order += [turned[(t + 1) * BT + b] for b in range(BT)]
        order += [rows[t * BT + b] for b in (0, 1)]
    order += [rows[(NT - 1) * BT + b] for b in (2, 3)]

    def tiles_of(w, first, n):
        part = np.asarray(w)[first * P:(first + n) * P]
        return part.reshape(n, P, KD, P).transpose(3, 0, 2, 1).reshape(P, -1)

    def moving(w, first, n):
        part = np.asarray(w)[first * P:(first + n) * P]
        return part.reshape(n * P, KD, P).transpose(2, 1, 0).reshape(P, -1)

    def by_input(w, first, n):
        part = np.asarray(w)[:, first * P:(first + n) * P]
        return part.reshape(D, n, P).transpose(2, 1, 0).reshape(P, -1)

    pairs = []
    for g in range(NG):
        pairs += [tiles_of(L0_attn_Wq, g * FT, FT), tiles_of(L0_attn_Wk, g * FT, FT),
                  moving(L0_attn_Wv, g * FT, FT), by_input(L0_attn_Wo, g * FT, FT)]
    for c in range(NC):
        for j in (2 * c, 2 * c + 1):
            pairs.append(np.concatenate([tiles_of(L0_ffn_w_gate, j, 1), tiles_of(L0_ffn_w_up, j, 1)], 1))
        pairs.append(by_input(L0_ffn_w_down, 2 * c, 2))

    by_token = np.zeros((B, S, MC), msk.dtype)
    by_token[:, :, :MB] = msk[:, None, :MB]
    for b in range(B):
        by_token[b, :, MB + b] = msk[b, MB]
    arrays = {
        "x": np.ascontiguousarray(np.asarray(x).reshape(NT, P, D).transpose(1, 0, 2)),
        "ctx": np.ascontiguousarray(np.stack(order)),
        "w": np.ascontiguousarray(np.stack(pairs)),
        "mask": np.ascontiguousarray(by_token.reshape(NT, P, MC).transpose(1, 0, 2)),
        "ext": np.ascontiguousarray(ctx[:, MB]),
        "ext_t": np.ascontiguousarray(ctx[:, MB].T.reshape(KD, P, B).transpose(1, 0, 2).reshape(P, KD * B)),
    }
    nc = bacc.Bacc("TRN2", target_bir_lowering=False, num_devices=1)
    args = [nc.dram_tensor(f"in_{n}", arr.shape, mybir.dt.from_np(arr.dtype), kind="ExternalInput").ap()
            for n, arr in arrays.items()]
    out = nc.dram_tensor("out", (B * S, D), F32, kind="ExternalOutput").ap()
    build(nc, *args, out)
    r = run_bass_kernel_spmd(nc, [{f"in_{n}": arr for n, arr in arrays.items()}], core_ids=[0])
    return r.results[0]["out"].reshape(B, S, D)
```

```python
from contextlib import ExitStack

import concourse.bass as bass
from concourse import mybir

ALU = mybir.AluOpType
ACT = mybir.ActivationFunctionType
AX = mybir.AxisListType
F32 = mybir.dt.float32
F32R = mybir.dt.float32r
U8 = mybir.dt.uint8

P = 128
B, S, D, M = 32, 32, 1024, 257
MB = M // P * P
MT = MB // P
NT = B * S // P
BT = P // S
KD = D // P
HALF = 512
UNIT = 2048
H, DK = 16, 64
HG = 4
NG = H // HG
FT = HG * DK // P
DH = 4096
NC = DH // 256
SLOTS = 4
MC = MB + B
PTW = MB + S
BIG = 1e30
CAUSAL_FILL = -3e38
EPS = 1e-5
CTX_UNITS = 2 * B
ATT_PAIRS = 4 * NG
CTX_USES = CTX_UNITS // SLOTS
ATT_USES = CTX_USES + ATT_PAIRS // SLOTS
FFN_SLOTS = 3


def build(nc, x_in, ctx_in, w_in, mask_in, ext_in, ext_t_in, out):
    stack = ExitStack()
    with stack:
        def sb(where, name, shape, dt=F32):
            return where.enter_context(nc.sbuf_tensor(name, shape, dt))

        def sem(name):
            return stack.enter_context(nc.semaphore(name))

        x = sb(stack, "x", [P, NT, D])
        raw = [sb(stack, f"raw{i}", [P, UNIT]) for i in range(SLOTS)]
        xn = [sb(stack, f"xn{i}", [P, D]) for i in range(2)]
        ident = sb(stack, "ident", [P, P])
        causal = sb(stack, "causal", [P, S])
        stats = sb(stack, "stats", [P, 2, 6])
        stats_next = sb(stack, "stats_next", [P, 2, 6])
        mean_var = sb(stack, "mean_var", [P, NT, 2])
        mean_var_now = sb(stack, "mean_var_now", [P, 2])
        rstd = sb(stack, "rstd", [P, NT, 1])
        mean_var_next = sb(stack, "mean_var_next", [P, 2])
        var_next = sb(stack, "var_next", [P, 1])
        rstd_next = sb(stack, "rstd_next", [P, 1])
        shift = sb(stack, "shift", [P, NT, 1])
        minus_half = sb(stack, "minus_half", [P, NT])

        a = ExitStack()
        cT_hi = [sb(a, f"cT_hi{i}", [P, 2, KD, MB], F32R) for i in range(2)]
        cT_lo = [sb(a, f"cT_lo{i}", [P, 2, KD, MB], F32R) for i in range(2)]
        cN_hi = [sb(a, f"cN_hi{i}", [P, MT, D], F32R) for i in range(2)]
        cN_lo = [sb(a, f"cN_lo{i}", [P, MT, D], F32R) for i in range(2)]
        xt_hi = sb(a, "xt_hi", [P, KD, P], F32R)
        xt_lo = sb(a, "xt_lo", [P, KD, P], F32R)
        pz_hi = sb(a, "pz_hi", [P, BT * PTW], F32R)
        pz_lo = sb(a, "pz_lo", [P, BT * PTW], F32R)
        pe_hi = sb(a, "pe_hi", [B, P], F32R)
        pe_lo = sb(a, "pe_lo", [B, P], F32R)
        ext_hi = sb(a, "ext_hi", [B, D], F32R)
        ext_lo = sb(a, "ext_lo", [B, D], F32R)
        extT_hi = sb(a, "extT_hi", [P, KD, B], F32R)
        extT_lo = sb(a, "extT_lo", [P, KD, B], F32R)
        mask = sb(a, "mask", [P, NT, MC], U8)
        valid = sb(a, "valid", [P, NT, 1])
        fill = sb(a, "fill", [P, MC])
        sc_sb = sb(a, "sc_sb", [P, MC])
        prob = sb(a, "prob", [P, MC])
        neg_top = sb(a, "neg_top", [P, 1])
        total = sb(a, "total", [P, 1])
        inv = sb(a, "inv", [P, 1])
        inv_valid = [sb(a, f"inv_valid{i}", [P, 1]) for i in range(2)]
        a.close()

        w_hi = [sb(stack, f"w_hi{i}", [P, UNIT], F32R) for i in range(2)]
        w_lo = [sb(stack, f"w_lo{i}", [P, UNIT], F32R) for i in range(2)]
        xT_hi = sb(stack, "xT_hi", [P, KD, NT * P], F32R)
        xT_lo = sb(stack, "xT_lo", [P, KD, NT * P], F32R)
        s = ExitStack()
        qT = sb(s, "qT", [P, FT, NT * P])
        kT = sb(s, "kT", [P, FT, NT * P])
        v = sb(s, "v", [P, NT, HG * DK])
        att = [sb(s, f"att{i}", [P, 2, 2, S]) for i in range(2)]
        att_p = [sb(s, f"att_p{i}", [P, HG, S]) for i in range(2)]
        att_z = [sb(s, f"att_z{i}", [P, HG, P]) for i in range(2)]
        att_neg = [sb(s, f"att_neg{i}", [P, HG]) for i in range(2)]
        att_sum = [sb(s, f"att_sum{i}", [P, HG]) for i in range(2)]
        att_inv = [sb(s, f"att_inv{i}", [P, HG]) for i in range(2)]
        inv_once = sb(s, "inv_once", [P, 1])
        o_sb = sb(s, "o_sb", [P, HG * DK])
        oT_hi = sb(s, "oT_hi", [P, FT, P], F32R)
        oT_lo = sb(s, "oT_lo", [P, FT, P], F32R)
        s.close()
        w_hi.append(sb(stack, "w_hi2", [P, UNIT], F32R))
        w_lo.append(sb(stack, "w_lo2", [P, UNIT], F32R))
        h_hi = sb(stack, "h_hi", [P, 2, NT * P], F32R)
        h_lo = sb(stack, "h_lo", [P, 2, NT * P], F32R)

        ps = stack.enter_context(nc.psum_tensor("ps", [P, 8, HALF], F32))

        x_full = [sem(f"x_full{i}") for i in range(2)]
        small_full = [sem(f"small_full{i}") for i in range(3)]
        stored = sem("stored")
        raw_full = [sem(f"raw_full{i}") for i in range(SLOTS)]
        split_done = [sem(f"split_done{i}") for i in range(SLOTS)]
        hi_done = sem("hi_done")
        const_done = sem("const_done")
        dve_own = sem("dve_own")
        ext_hi_done = sem("ext_hi_done")
        ext_done = sem("ext_done")
        next_var_ready = sem("next_var_ready")
        next_scale_ready = sem("next_scale_ready")
        var_ready = sem("var_ready")
        pow_done = sem("pow_done")
        mean_scaled = sem("mean_scaled")
        scale_ready = sem("scale_ready")
        xn_ready = sem("xn_ready")
        xn_odd_ready = sem("xn_odd_ready")
        xt_psum = sem("xt_psum")
        xt_hi_done = sem("xt_hi_done")
        xt_ready = sem("xt_ready")
        scores_done = sem("scores_done")
        scores_read = sem("scores_read")
        top_ready = sem("top_ready")
        exp_done = sem("exp_done")
        pt_psum = sem("pt_psum")
        pt_hi_done = sem("pt_hi_done")
        pt_ready = sem("pt_ready")
        ctx_used = sem("ctx_used")
        readout_done = sem("readout_done")
        readout_free = sem("readout_free")
        q_done = sem("q_done")
        k_done = sem("k_done")
        v_done = sem("v_done")
        q_kept = sem("q_kept")
        k_kept = sem("k_kept")
        v_kept = sem("v_kept")
        att_done = sem("att_done")
        att_read = sem("att_read")
        att_top_ready = sem("att_top_ready")
        att_exp = sem("att_exp")
        att_turned = sem("att_turned")
        z_zero = sem("z_zero")
        pv_done = sem("pv_done")
        o_ready = sem("o_ready")
        oT_psum = sem("oT_psum")
        oT_hi_done = sem("oT_hi_done")
        oT_ready = sem("oT_ready")
        wo_done = sem("wo_done")
        wo_free = sem("wo_free")
        gu_done = sem("gu_done")
        silu_done = sem("silu_done")
        h_done = sem("h_done")
        h_hi_done = sem("h_hi_done")
        h_ready = sem("h_ready")
        down_done = sem("down_done")
        down_added = sem("down_added")

        def sg(half):
            return xn[0][:, half * HALF:(half + 1) * HALF]

        def gf(half):
            return xn[1][:, half * HALF:(half + 1) * HALF]

        block = stack.enter_context(nc.Block())

        def turned_unit(t, b):
            if isinstance(t, int) and t == 0:
                return b, b, 0
            return (t * 8 + (b - 4), b, t * 2 - 1) if b < 2 else (t * 8 + (b - 2), b - 2, t * 2)

        def rows_unit(t, b):
            if isinstance(t, int) and t == NT - 1:
                return CTX_UNITS - 4 + b, b, CTX_USES - 1
            return (t * 8 + (6 + b), 2 + b, t * 2 + 1) if b < 2 else (t * 8 + (8 + b), b, t * 2 + 2)

        def scales_of(n, t):
            return (n - 1) * NT + max(t + 1, NT - 2 if n == 1 else 0)

        TURN_BANKS = (0, 6, 4, 2, 6, 4, 6, 4)
        TURN_AFTER = (None, None, None, None, 1, 2, 4, 5)

        @block.sync
        def _(sync):
            sync.dma_start(x[:, 0, :], x_in[:, 0, :]).then_inc(x_full[0], 16)
            for i in range(SLOTS):
                sync.dma_start(raw[i][:, :], ctx_in[i]).then_inc(raw_full[i], 16)
            with sync.Fori(1, CTX_USES) as u:
                for i in range(SLOTS):
                    sync.wait_ge(split_done[i], u)
                    sync.dma_start(raw[i][:, :], ctx_in[u * SLOTS + i]).then_inc(raw_full[i], 16)
            with sync.Fori(0, NG) as g:
                for i in range(SLOTS):
                    sync.wait_ge(split_done[i], g + CTX_USES)
                    sync.dma_start(raw[i][:, :], w_in[g * SLOTS + i]).then_inc(raw_full[i], 16)
            with sync.Fori(0, NC) as c:
                for i in range(FFN_SLOTS):
                    sync.wait_ge(split_done[i], c + ATT_USES)
                    sync.dma_start(raw[i][:, :], w_in[c * FFN_SLOTS + (ATT_PAIRS + i)])\
                        .then_inc(raw_full[i], 16)
            for t in range(NT):
                sync.wait_ge(down_added, 2 * NT * (NC - 1) + 2 * t + 2)
                sync.dma_start(out[t * P:(t + 1) * P, :], x[:, t, :]).then_inc(stored, 16)
            sync.wait_ge(stored, 16 * NT)

        @block.gpsimd
        def _(pool):
            pool.dma_start(mask[:, :, :], mask_in).then_inc(small_full[0], 16)
            pool.memset(ident[:, :], 0.0).then_inc(const_done, 1)
            pool.memset(causal[:, :], 0.0).then_inc(const_done, 1)
            pool.memset(minus_half[:, :], -0.5)
            pool.memset(pz_hi[:, :].bitcast(F32), 0.0).then_inc(const_done, 1)
            pool.memset(pz_lo[:, :].bitcast(F32), 0.0).then_inc(const_done, 1)
            pool.wait_ge(const_done, 4)
            pool.affine_select(out=ident[:, :], in_=ident[:, :], compare_op=ALU.not_equal, fill=1.0,
                               base=0, pattern=[[-1, P]], channel_multiplier=1).then_inc(const_done, 1)
            for b in range(BT):
                q = slice(b * S, (b + 1) * S)
                pool.wait_ge(const_done, 5 + b)
                pool.affine_select(out=causal[q, :], in_=causal[q, :], compare_op=ALU.is_ge,
                                   fill=CAUSAL_FILL, base=0, pattern=[[-1, S]],
                                   channel_multiplier=1).then_inc(const_done, 1)

            def lo(unit, dst, hi):
                n, slot, _ = unit
                pool.wait_ge(hi_done, n + 1)
                pool.tensor_tensor(dst, raw[slot][:, :], hi.bitcast(F32), ALU.subtract)\
                    .then_inc(split_done[slot], 1)

            def turned(t):
                lo(turned_unit(t, 3), flat(cT_lo[1][:, 1]), flat(cT_hi[1][:, 1]))

            def rows(t):
                lo(rows_unit(t, 3), flat(cN_lo[1][:, :, :]), flat(cN_hi[1][:, :, :]))

            def next_scale(t):
                pool.wait_ge(next_var_ready, t + 1)
                pool.tensor_tensor(rstd_next[:, :], var_next[:, :], minus_half[:, 0:1], ALU.pow)\
                    .then_inc(next_scale_ready, 1)

            def scales(n, t, tiles=1):
                part = slice(t + 1 - tiles, t + 1)
                count = (n - 1) * NT + t + 1
                pool.wait_ge(var_ready, count)
                pool.tensor_tensor(rstd[:, part, 0], mean_var[:, part, 1],
                                   minus_half[:, 0:tiles], ALU.pow).then_inc(pow_done, tiles)
                pool.wait_ge(pow_done, count)
                pool.tensor_tensor(shift[:, part, 0], mean_var[:, part, 0], rstd[:, part, 0], ALU.mult)\
                    .then_inc(mean_scaled, tiles)
                pool.wait_ge(mean_scaled, count)
                pool.tensor_scalar(shift[:, part, 0], shift[:, part, 0], -1.0, 1.0, ALU.mult, ALU.mult)\
                    .then_inc(scale_ready, tiles)

            pool.wait_ge(const_done, 5 + BT)
            next_scale(0)
            turned(0)
            next_scale(1)
            turned(1)
            next_scale(2)
            rows(0)
            with pool.Fori(2, NT - 1) as t:
                turned(t)
                next_scale(t + 1)
                rows(t - 1)
            turned(NT - 1)
            rows(NT - 2)
            scales(1, NT - 3, NT - 2)
            rows(NT - 1)
            scales(1, NT - 2)

            def weights(slot, pair, wslot):
                pool.wait_ge(hi_done, pair + (CTX_UNITS + 1))
                pool.tensor_tensor(w_lo[wslot][:, :], raw[slot][:, :], w_hi[wslot][:, :].bitcast(F32),
                                   ALU.subtract).then_inc(split_done[slot], 1)

            weights(0, 0, 0)
            scales(1, NT - 1)
            pool.wait_ge(wo_free, 1)
            for i in range(2):
                pool.memset(att_z[i][:, :, :], 0.0).then_inc(z_zero, 1)
            with pool.Fori(0, NG - 1) as g:
                for i in range(SLOTS):
                    weights((i + 1) % SLOTS, g * SLOTS + (i + 1), (i + 1) % 2)
            for i in range(SLOTS):
                weights((i + 1) % SLOTS, (NG - 1) * SLOTS + i + 1, (i + 1) % 2)
            for t in range(NT - 1):
                scales(2, t)
            weights(1, ATT_PAIRS + 1, 1)
            scales(2, NT - 1)
            for i in (2, 3):
                weights(i % FFN_SLOTS, ATT_PAIRS + i, i % FFN_SLOTS)
            with pool.Fori(1, NC - 1) as c:
                for i in range(FFN_SLOTS):
                    k = (i + 1) % FFN_SLOTS
                    weights(k, c * FFN_SLOTS + (ATT_PAIRS + i + 1), k)
            for i in (1, 2):
                weights(i, (NC - 1) * FFN_SLOTS + ATT_PAIRS + i, i)

        @block.scalar
        def _(act):
            act.dma_start(xn[1][0:B, :], ext_in).then_inc(small_full[1], 16)
            act.dma_start(prob[:, 0:KD * B], ext_t_in).then_inc(small_full[2], 16)

            def hi(unit, dst):
                _, slot, use = unit
                act.wait_ge(raw_full[slot], (use + 1) * 16)
                act.activation(dst, raw[slot][:, :], ACT.Copy).then_inc(hi_done, 1)

            def turned(t, b):
                hi(turned_unit(t, b), flat(cT_hi[b // 2][:, b % 2]))

            def rows(t, b):
                hi(rows_unit(t, b), flat(cN_hi[b % 2][:, :, :]))

            act.wait_ge(small_full[1], 16)
            act.activation(ext_hi[:, :], xn[1][0:B, :], ACT.Copy).then_inc(ext_hi_done, 1)
            act.wait_ge(small_full[2], 16)
            act.activation(flat(extT_hi[:, :, :]), prob[:, 0:KD * B], ACT.Copy).then_inc(ext_hi_done, 1)
            for b in range(BT):
                turned(0, b)

            def tile(t, parity, first=False, last=False):
                if not last:
                    act.dma_start(x[:, t + 1, :], x_in[:, t + 1, :]).then_inc(x_full[1 - parity], 16)
                act.wait_ge(xt_psum, t + 1)
                act.activation(flat(xt_hi[:, :, :]), flat(ps[:, 0:2, :]), ACT.Copy).then_inc(xt_hi_done, 1)
                if not first:
                    act.wait_ge(scores_done, t * 2)
                    turned(t, 2)
                    turned(t, 3)
                    for b in (2, 3):
                        act.wait_ge(ctx_used, t * 4 + (b - 5))
                        rows(t - 1, b)
                if not last:
                    act.wait_ge(scores_done, t * 2 + 1)
                    turned(t + 1, 0)
                    turned(t + 1, 1)
                act.wait_ge(top_ready, t + 1)
                act.activation(prob[:, :], sc_sb[:, :], ACT.Exp, bias=neg_top[:, 0:1],
                               accum_out=total[:, 0:1]).then_inc(exp_done, 1)
                for b in (0, 1):
                    if not first:
                        act.wait_ge(ctx_used, t * 4 + (b - 1))
                    rows(t, b)
                act.wait_ge(pt_psum, t + 1)
                if first:
                    act.wait_ge(const_done, 4)
                act.activation(blocks(pz_hi), turned_psum(ps), ACT.Copy)
                act.activation(pe_hi[:, :], ps[0:B, 5, MB:MB + P], ACT.Copy).then_inc(pt_hi_done, 1)

            tile(0, 0, first=True)
            tile(1, 1)
            with act.Fori(2, NT - 2, 2) as t:
                for parity in range(2):
                    tile(t + parity, parity)
            tile(NT - 2, 0)
            tile(NT - 1, 1, last=True)
            for b in (2, 3):
                act.wait_ge(ctx_used, 4 * (NT - 1) + b - 1)
                rows(NT - 1, b)

            def weights(slot, use, wslot):
                act.wait_ge(raw_full[slot], (use + 1) * 16)
                act.activation(w_hi[wslot][:, :], raw[slot][:, :], ACT.Copy).then_inc(hi_done, 1)

            act.wait_ge(scores_done, 2 * NT)
            weights(0, CTX_USES, 0)

            def normalise(n, t):
                act.wait_ge(scale_ready, scales_of(n, t))
                if t > 1:
                    act.wait_ge(xt_psum, n * NT + t - 1)
                act.activation(xn[1][:, :], x[:, t, :], ACT.Identity, bias=shift[:, t, :],
                               scale=rstd[:, t, :]).then_inc(xn_odd_ready, 1)

            def norm(n):
                normalise(n, 1)
                for t in range(NT):
                    act.wait_ge(xt_psum, n * NT + t + 1)
                    act.activation(xT_hi[:, :, t * P:(t + 1) * P], tile_psum(ps, TURN_BANKS[t]), ACT.Copy)\
                        .then_inc(xt_hi_done, 1)
                    if t % 2 and t + 2 < NT:
                        normalise(n, t + 2)

            norm(1)

            def group(g):
                def split(k):
                    if k == 0:
                        act.wait_ge(wo_free, g * 8 + 2)
                    else:
                        act.wait_ge((q_done, k_done, v_done)[k - 1], (g + 1) * (4, 4, 8)[k - 1])
                    weights((k + 1) % 4, g + (CTX_USES + (k + 1) // 4), (k + 1) % 2)

                def exps(st):
                    act.wait_ge(att_top_ready, g * 8 + (st + 1))
                    rowsof = flat3(att[st % 2])
                    for h in range(HG):
                        ins = act.activation(att_p[st % 2][:, h, :], rowsof[:, h * S:(h + 1) * S], ACT.Exp,
                                             bias=att_neg[st % 2][:, h:h + 1],
                                             accum_out=att_sum[st % 2][:, h:h + 1])
                    ins.then_inc(att_exp, 1)

                split(0)
                for j in range(2 * FT):
                    act.wait_ge(q_done, g * 4 + (j + 1))
                    act.activation(qT[:, j % 2, (j // 2) * HALF:(j // 2 + 1) * HALF],
                                   ps[:, j, :], ACT.Copy, scale=DK ** -0.5).then_inc(q_kept, 1)
                split(1)
                split(2)
                for t in range(NT):
                    if t == NT - 1:
                        exps(0)
                    act.wait_ge(v_done, g * 8 + (t + 1))
                    act.activation(v[:, t, :], ps[:, t, 0:HG * DK], ACT.Copy).then_inc(v_kept, 1)
                for st in range(1, NT + 2):
                    if st >= 2:
                        act.wait_ge(oT_psum, g * 8 + (st - 1))
                        act.activation(flat(oT_hi[:, :, :]), ps[:, 5, 0:FT * P], ACT.Copy)\
                            .then_inc(oT_hi_done, 1)
                    if st < NT:
                        exps(st)
                    if st == 2:
                        split(3)

            with act.Fori(0, NG - 1) as g:
                group(g)
            group(NG - 1)
            act.wait_ge(wo_done, NG * NT)
            weights(1, ATT_USES, 1)
            norm(2)

            def chunk(c, first=False, last=False):
                for k in range(3):
                    if not (first and k == 0) and not (last and k == 2):
                        if k == 0:
                            act.wait_ge(gu_done, c * 4)
                        elif k == 2:
                            act.wait_ge(gu_done, c * 4 + 2)
                        elif not first:
                            act.wait_ge(down_done, c * 16)
                        nxt = (k + 1) % 3
                        weights(nxt, c + (ATT_USES + (k + 1) // 3), nxt)
                    if k < 2:
                        for half in range(2):
                            n = 2 * k + half
                            act.wait_ge(gu_done, c * 4 + (n + 1))
                            act.activation(sg(half), ps[:, 2 * n, :], ACT.Silu).then_inc(silu_done, 1)
                            act.wait_ge(h_done, c * 4 + (n + 1))
                            act.activation(h_hi[:, k, half * HALF:(half + 1) * HALF], gf(half), ACT.Copy)\
                                .then_inc(h_hi_done, 1)

            chunk(0, first=True)
            with act.Fori(1, NC - 1) as c:
                chunk(c)
            chunk(NC - 1, last=True)

        @block.tensor
        def _(pe):
            def three(dst, stat, moving, start, stop):
                pe.matmul(dst, stat[0], moving[0], start=start, stop=False)
                pe.matmul(dst, stat[0], moving[1], start=False, stop=False)
                return pe.matmul(dst, stat[1], moving[0], start=False, stop=stop)

            def unit_ready(unit):
                _, slot, use = unit
                pe.wait_ge(split_done[slot], use + 1)

            def turn(src, banks):
                for k in range(KD):
                    mm = pe.transpose(ps[:, banks + k // 4, (k % 4) * P:(k % 4 + 1) * P],
                                      src[:, k * P:(k + 1) * P], ident[:, :])
                mm.then_inc(xt_psum, 1)

            def readout(t, parity, batches):
                bank = (6, 2)[parity]
                for b in batches:
                    unit_ready(rows_unit(t, b))
                    for half in range(2):
                        for m in range(MT):
                            col = b * MB + m * P
                            mm = three(ps[:, bank + half, :],
                                       (pz_hi[:, col:col + P], pz_lo[:, col:col + P]),
                                       (cN_hi[b % 2][:, m, half * HALF:(half + 1) * HALF],
                                        cN_lo[b % 2][:, m, half * HALF:(half + 1) * HALF]),
                                       start=(b == 0 and m == 0), stop=False)
                    mm.then_inc(ctx_used, 1)
                if 3 in batches:
                    for half in range(2):
                        mm = three(ps[:, bank + half, :], (pe_hi[:, :], pe_lo[:, :]),
                                   (ext_hi[:, half * HALF:(half + 1) * HALF],
                                    ext_lo[:, half * HALF:(half + 1) * HALF]), start=False, stop=True)
                    mm.then_inc(readout_done, 1)

            def tile(t, parity, first=False):
                pe.wait_ge(xn_ready, t + 1)
                if not first:
                    pe.wait_ge(scores_read, t)
                turn(xn[0], 0)
                if not first:
                    pe.wait_ge(pt_ready, t)
                    pe.wait_ge(readout_free, t)
                    readout(t - 1, 1 - parity, (0, 1))
                pe.wait_ge(xt_ready, t + 1)
                if first:
                    pe.wait_ge(ext_done, 1)
                for k in range(KD):
                    three(ps[:, 5, MB + P:MB + P + B], (xt_hi[:, k, :], xt_lo[:, k, :]),
                          (extT_hi[:, k, :], extT_lo[:, k, :]), start=(k == 0), stop=(k == KD - 1))
                for pair in range(2):
                    for b in (2 * pair, 2 * pair + 1):
                        unit_ready(turned_unit(t, b))
                    for k in range(KD):
                        mm = three(ps[:, pair, :].rearrange("p (b m) -> p b m", b=2),
                                   (xt_hi[:, k, :], xt_lo[:, k, :]),
                                   (cT_hi[pair][:, :, k, :], cT_lo[pair][:, :, k, :]),
                                   start=(k == 0), stop=(k == KD - 1))
                    mm.then_inc(scores_done, 1)
                if not first:
                    readout(t - 1, 1 - parity, (2, 3))
                pe.wait_ge(exp_done, t + 1)
                for m in range(MT):
                    pe.transpose(ps[:, 5, m * P:(m + 1) * P], prob[:, m * P:(m + 1) * P], ident[:, :])
                pe.transpose(ps[0:B, 5, MB:MB + P], prob[:, MB:MC], ident[:, :]).then_inc(pt_psum, 1)

            pe.wait_ge(const_done, 5)
            tile(0, 0, first=True)
            tile(1, 1)
            with pe.Fori(2, NT - 2, 2) as t:
                for parity in range(2):
                    tile(t + parity, parity)
            tile(NT - 2, 0)
            tile(NT - 1, 1)

            def norm_tile(n, t):
                if t % 2:
                    pe.wait_ge(xn_odd_ready, (n - 1) * NT // 2 + t // 2 + 1)
                else:
                    pe.wait_ge(xn_ready, NT + (n - 1) * NT // 2 + t // 2 + 1)
                if TURN_AFTER[t] is not None:
                    pe.wait_ge(xt_ready, n * NT + TURN_AFTER[t] + 1)
                turn(xn[t % 2], TURN_BANKS[t])

            pe.wait_ge(pt_ready, NT)
            pe.wait_ge(readout_free, NT)
            readout(NT - 1, 1, (0, 1))
            pe.wait_ge(readout_free, NT + 1)
            for t in range(2):
                norm_tile(1, t)
            readout(NT - 1, 1, (2, 3))
            norm_tile(1, 2)
            pe.wait_ge(readout_free, NT + 2)
            norm_tile(1, 3)

            def stationary(slot, unit, k):
                at = (unit * KD + k) * P
                return w_hi[slot][:, at:at + P], w_lo[slot][:, at:at + P]

            def tokens(k, at, n):
                return xT_hi[:, k, at:at + n], xT_lo[:, k, at:at + n]

            def scores(g, st):
                for h in range(HG):
                    r = slice((h % 2) * DK, (h % 2 + 1) * DK)
                    mm = pe.matmul(ps[:, h % 2, (h // 2) * P:(h // 2 + 1) * P],
                                   qT[r, h // 2, st * P:(st + 1) * P],
                                   kT[r, h // 2, st * P:(st + 1) * P], start=True, stop=True)
                mm.then_inc(att_done, 1)

            def group(g, first=False):
                for kind, done in ((0, q_done), (1, k_done)):
                    pe.wait_ge(split_done[kind], g + (CTX_USES + 1))
                    for j in range(2 * FT):
                        if first and kind == 0:
                            pe.wait_ge(xt_ready, NT + (4, 4, 8, 8)[j])
                        if j == 2:
                            pe.wait_ge(wo_free, g * 8 + 2)
                        for k in range(KD):
                            mm = three(ps[:, 4 * kind + j, :], stationary(kind, j % 2, k),
                                       tokens(k, (j // 2) * HALF, HALF), start=(k == 0), stop=(k == KD - 1))
                        mm.then_inc(done, 1)
                        if first and kind == 0 and j < 2:
                            norm_tile(1, 4 + 2 * j)
                            norm_tile(1, 5 + 2 * j)
                pe.wait_ge(split_done[2], g + (CTX_USES + 1))
                W = HG * DK
                for t in range(NT):
                    if t < 4:
                        pe.wait_ge(q_kept, g * 4 + (t + 1))
                    else:
                        pe.wait_ge(k_kept, g * 4 + (t - 3))
                    if t == NT - 1:
                        pe.wait_ge(q_kept, g * 4 + 4)
                        pe.wait_ge(k_kept, g * 4 + 4)
                        pe.wait_ge(v_kept, g * 8 + 2)
                        scores(g, 0)
                    for k in range(KD):
                        mm = three(ps[:, t, 0:W], tokens(k, t * P, P),
                                   (w_hi[0][:, k * W:(k + 1) * W], w_lo[0][:, k * W:(k + 1) * W]),
                                   start=(k == 0), stop=(k == KD - 1))
                    mm.then_inc(v_done, 1)
                pe.wait_ge(v_kept, g * 8 + 8)
                for st in range(1, NT + 2):
                    if st >= 2:
                        pe.wait_ge(o_ready, g * 8 + (st - 1))
                        for f in range(FT):
                            mm = pe.transpose(ps[:, 5, f * P:(f + 1) * P], o_sb[:, f * P:(f + 1) * P],
                                              ident[:, :])
                        mm.then_inc(oT_psum, 1)
                    if st < NT:
                        pe.wait_ge(att_read, g * 8 + st)
                        scores(g, st)
                    if 1 <= st <= NT:
                        pe.wait_ge(att_turned, g * 8 + st)
                        for h in range(HG):
                            mm = pe.matmul(ps[:, 4, h * DK:(h + 1) * DK], att_z[(st - 1) % 2][:, (h % 2) * 2 + h // 2, :],
                                           v[:, st - 1, h * DK:(h + 1) * DK], start=True, stop=True)
                        mm.then_inc(pv_done, 1)
                    if st >= 2:
                        if st == 2:
                            pe.wait_ge(split_done[3], g + (CTX_USES + 1))
                        pe.wait_ge(oT_ready, g * 8 + (st - 1))
                        pe.wait_ge(wo_free, g * 8 + (st - 1))
                        for f in range(FT):
                            for half in range(2):
                                at = f * D + half * HALF
                                mm = three(ps[:, (6, 2)[st % 2] + half, :], (oT_hi[:, f, :], oT_lo[:, f, :]),
                                           (w_hi[1][:, at:at + HALF], w_lo[1][:, at:at + HALF]),
                                           start=(f == 0), stop=(f == FT - 1))
                        mm.then_inc(wo_done, 1)

            group(0, first=True)
            with pe.Fori(1, NG) as g:
                group(g)
            norm_tile(2, 0)
            pe.wait_ge(wo_free, NG * 8 + 1)
            norm_tile(2, 1)
            norm_tile(2, 2)
            pe.wait_ge(wo_free, NG * 8 + 2)
            norm_tile(2, 3)

            def chunk(c, first=False):
                for k in range(2):
                    pe.wait_ge(split_done[k], c + (ATT_USES + 1))
                    for half in range(2):
                        n = 2 * k + half
                        if not first:
                            pe.wait_ge(down_added, (c - 1) * 16 + (8 + 2 * n + 2))
                        if first and k == 0:
                            pe.wait_ge(xt_ready, 2 * NT + 4 * (half + 1))
                        for u in range(2):
                            for kk in range(KD):
                                mm = three(ps[:, 2 * n + u, :], stationary(k, u, kk),
                                           tokens(kk, half * HALF, HALF), start=(kk == 0),
                                           stop=(kk == KD - 1))
                            if u:
                                mm.then_inc(gu_done, 1)
                            if first and n == 0:
                                norm_tile(2, 4 + 2 * u)
                                norm_tile(2, 5 + 2 * u)
                pe.wait_ge(split_done[2], c + (ATT_USES + 1))
                for i in range(2 * NT):
                    t, half = i // 2, i % 2
                    if i == 0:
                        pe.wait_ge(h_ready, c * 4 + 3)
                    if i == NT:
                        pe.wait_ge(h_ready, c * 4 + 4)
                    if i < 8:
                        pe.wait_ge(h_done, c * 4 + (i // 2 + 1))
                    else:
                        pe.wait_ge(down_added, c * 16 + (i - 7))
                    for k in range(2):
                        at = k * D + half * HALF
                        mm = three(ps[:, i % 8, :],
                                   (h_hi[:, k, t * P:(t + 1) * P], h_lo[:, k, t * P:(t + 1) * P]),
                                   (w_hi[2][:, at:at + HALF], w_lo[2][:, at:at + HALF]),
                                   start=(k == 0), stop=(k == 1))
                    mm.then_inc(down_done, 1)

            chunk(0, first=True)
            with pe.Fori(1, NC) as c:
                chunk(c)

        @block.vector
        def _(dve):
            own = [0, 0]

            class at:
                base = 0

            def mark(ins):
                own[0] += 1
                ins.then_inc(dve_own, 1)

            def settle():
                dve.wait_ge(dve_own, at.base + own[0])

            def lo(unit, dst, hi):
                n, slot, _ = unit
                dve.wait_ge(hi_done, n + 1)
                dve.tensor_tensor(dst, raw[slot][:, :], hi.bitcast(F32), ALU.subtract)\
                    .then_inc(split_done[slot], 1)

            def turned(t, b):
                lo(turned_unit(t, b), flat(cT_lo[b // 2][:, b % 2]), flat(cT_hi[b // 2][:, b % 2]))

            def rows(t, b):
                lo(rows_unit(t, b), flat(cN_lo[b % 2][:, :, :]), flat(cN_hi[b % 2][:, :, :]))

            def both_stats(dst, t):
                for half in range(2):
                    ins = dve.bn_stats(dst[:, half, :], x[:, t, half * HALF:(half + 1) * HALF])
                mark(ins)

            def tile_stats(t):
                both_stats(stats, t)
                settle()
                mark(dve.bn_aggr(mean_var[:, t, :], stats[:, :, :]))
                settle()
                dve.tensor_scalar(mean_var[:, t, 1:2], mean_var[:, t, 1:2], EPS, None, ALU.add)\
                    .then_inc(var_ready, 1)

            def next_normalise(t):
                dve.wait_ge(next_scale_ready, t + 1)
                dve.tensor_scalar(xn[0][:, :], x[:, t, :], mean_var_next[:, 0:1], rstd_next[:, :],
                                  ALU.subtract, ALU.mult).then_inc(xn_ready, 1)

            def normalise(n, t):
                dve.wait_ge(scale_ready, scales_of(n, t))
                dve.tensor_scalar(xn[0][:, :], x[:, t, :], mean_var[:, t, 0:1], rstd[:, t, :],
                                  ALU.subtract, ALU.mult).then_inc(xn_ready, 1)

            dve.wait_ge(x_full[0], 16)
            both_stats(stats_next, 0)
            settle()
            mark(dve.bn_aggr(mean_var_next[:, :], stats_next[:, :, :]))
            settle()
            dve.tensor_scalar(var_next[:, :], mean_var_next[:, 1:2], EPS, None, ALU.add)\
                .then_inc(next_var_ready, 1)
            dve.wait_ge(ext_hi_done, 2)
            dve.tensor_tensor(ext_lo[:, :], xn[1][0:B, :], ext_hi[:, :].bitcast(F32), ALU.subtract)
            dve.tensor_tensor(flat(extT_lo[:, :, :]), prob[:, 0:KD * B], flat(extT_hi[:, :, :]).bitcast(F32),
                              ALU.subtract).then_inc(ext_done, 1)
            next_normalise(0)
            for b in range(3):
                turned(0, b)
            dve.wait_ge(small_full[0], 16)
            mark(dve.tensor_reduce(valid[:, :, 0], mask[:, :, :], AX.X, ALU.max))

            def add_readout(t, parity):
                dve.wait_ge(readout_done, t + 1)
                settle()
                for half in range(2):
                    part = x[:, t, half * HALF:(half + 1) * HALF]
                    ins = dve.scalar_tensor_tensor(out=part, in0=ps[:, (6, 2)[parity] + half, :],
                                                   scalar=inv_valid[parity][:, 0:1], in1=part,
                                                   op0=ALU.mult, op1=ALU.add)
                ins.then_inc(readout_free, 1)

            def tile(t, parity, early=False, first=False, last=False):
                dve.wait_ge(xt_hi_done, t + 1)
                dve.tensor_tensor(flat(xt_lo[:, :, :]), flat(ps[:, 0:2, :]),
                                  flat(xt_hi[:, :, :]).bitcast(F32), ALU.subtract).then_inc(xt_ready, 1)
                if first:
                    dve.memset(inv_valid[1][:, :], 0.0).then_inc(readout_free, 2)
                if not last:
                    dve.wait_ge(x_full[1 - parity], (t + (2 + parity)) * 8)
                mark(dve.tensor_scalar(fill[:, :], mask[:, t, :], BIG, -BIG, ALU.mult, ALU.add))
                if not last:
                    both_stats(stats_next, t + 1)
                if not early:
                    add_readout(t - 2, parity)
                else:
                    settle()
                if not last:
                    mark(dve.bn_aggr(mean_var_next[:, :], stats_next[:, :, :]))
                settle()
                if not early:
                    dve.wait_ge(readout_free, t + 1)
                if not first:
                    turned(t, 2)
                if not last:
                    dve.tensor_scalar(var_next[:, :], mean_var_next[:, 1:2], EPS, None, ALU.add)\
                        .then_inc(next_var_ready, 1)
                if not early:
                    both_stats(stats, t - 2)
                    settle()
                if not first:
                    rows(t - 1, 2)
                if not early:
                    mark(dve.bn_aggr(mean_var_now[:, :], stats[:, :, :]))
                    settle()
                if not last:
                    next_normalise(t + 1)
                    turned(t + 1, 0)
                if not early:
                    mark(dve.tensor_copy(mean_var[:, t - 2, :], mean_var_now[:, :]))
                dve.wait_ge(scores_done, t * 2 + 2)
                for b in range(BT):
                    q = slice(b * S, (b + 1) * S)
                    dve.scalar_tensor_tensor(out=sc_sb[q, 0:MB],
                                             in0=ps[q, b // 2, (b % 2) * MB:(b % 2 + 1) * MB],
                                             scalar=D ** -0.5, in1=mask[q, t, 0:MB],
                                             op0=ALU.mult, op1=ALU.mult)
                dve.scalar_tensor_tensor(out=sc_sb[:, MB:MC], in0=ps[:, 5, MB + P:MB + P + B],
                                         scalar=D ** -0.5, in1=mask[:, t, MB:MC], op0=ALU.mult,
                                         op1=ALU.mult).then_inc(scores_read, 1)
                dve.wait_ge(scores_read, t + 1)
                settle()
                mark(dve.tensor_tensor(sc_sb[:, :], sc_sb[:, :], fill[:, :], ALU.add))
                settle()
                dve.tensor_reduce(neg_top[:, :], sc_sb[:, :], AX.X, ALU.max, negate=True)\
                    .then_inc(top_ready, 1)
                if not last:
                    turned(t + 1, 1)
                dve.wait_ge(exp_done, t + 1)
                mark(dve.reciprocal(inv[:, :], total[:, :]))
                settle()
                mark(dve.tensor_scalar(inv_valid[parity][:, :], inv[:, :], valid[:, t, :], None, ALU.mult))
                rows(t, 0)
                dve.wait_ge(pt_hi_done, t + 1)
                if first:
                    dve.wait_ge(const_done, 4)
                dve.tensor_tensor(blocks(pz_lo), turned_psum(ps), blocks(pz_hi).bitcast(F32), ALU.subtract)
                dve.tensor_tensor(pe_lo[:, :], ps[0:B, 5, MB:MB + P], pe_hi[:, :].bitcast(F32),
                                  ALU.subtract).then_inc(pt_ready, 1)
                rows(t, 1)

            tile(0, 0, early=True, first=True)
            tile(1, 1, early=True)
            start = own[0]
            with dve.Fori(2, NT - 2, 2) as t:
                at.base = (t - 2) * (TWO_TILE_MARKS // 2)
                for parity in range(2):
                    tile(t + parity, parity)
                assert own[0] - start == TWO_TILE_MARKS, own[0] - start
            at.base = TWO_TILE_MARKS * ((NT - 4) // 2 - 1)
            tile(NT - 2, 0)
            tile(NT - 1, 1, last=True)

            def turned_lo(n, t):
                dve.wait_ge(xt_hi_done, n * NT + t + 1)
                dve.tensor_tensor(xT_lo[:, :, t * P:(t + 1) * P], tile_psum(ps, TURN_BANKS[t]),
                                  xT_hi[:, :, t * P:(t + 1) * P].bitcast(F32), ALU.subtract)\
                    .then_inc(xt_ready, 1)

            settle()
            dve.tensor_scalar(mean_var[:, 0:NT - 2, 1], mean_var[:, 0:NT - 2, 1], EPS, None, ALU.add)\
                .then_inc(var_ready, NT - 2)
            rows(NT - 1, 2)
            add_readout(NT - 2, 0)
            dve.wait_ge(readout_free, NT + 1)
            tile_stats(NT - 2)
            normalise(1, 0)
            add_readout(NT - 1, 1)
            dve.wait_ge(readout_free, NT + 2)
            dve.memset(inv_once[:, :], 0.0).then_inc(wo_free, 2)
            tile_stats(NT - 1)

            def norm(n):
                for t in range(NT):
                    if t % 2 == 0 and t + 2 < NT:
                        dve.wait_ge(xt_psum, n * NT + t + 1)
                        normalise(n, t + 2)
                    turned_lo(n, t)

            norm(1)

            def group(g, last=False):
                for j in range(2 * FT):
                    dve.wait_ge(k_done, g * 4 + (j + 1))
                    dve.tensor_copy(kT[:, j % 2, (j // 2) * HALF:(j // 2 + 1) * HALF], ps[:, 4 + j, :])\
                        .then_inc(k_kept, 1)
                for st in range(NT + 2):
                    two = st % 2
                    if st >= 2:
                        dve.wait_ge(oT_hi_done, g * 8 + (st - 1))
                        dve.tensor_tensor(flat(oT_lo[:, :, :]), ps[:, 5, 0:FT * P],
                                          flat(oT_hi[:, :, :]).bitcast(F32), ALU.subtract)\
                            .then_inc(oT_ready, 1)
                    if st < NT:
                        dve.wait_ge(att_done, g * 8 + (st + 1))
                        for b in range(BT):
                            q = slice(b * S, (b + 1) * S)
                            src = ps[q, 0:2, 0:2 * P].rearrange("p e (h k) -> p e h k", h=2)
                            ins = dve.tensor_tensor(
                                att[two][q, :, :, :], src[:, :, :, b * S:(b + 1) * S],
                                causal[q, :].unsqueeze(1).unsqueeze(1).broadcast_to([S, 2, 2, S]), ALU.add)
                        ins.then_inc(att_read, 1)
                        dve.wait_ge(att_read, g * 8 + (st + 1))
                        dve.tensor_reduce(att_neg[two][:, :],
                                          flat3(att[two]).rearrange("p (h k) -> p h k", h=HG), AX.X,
                                          ALU.max, negate=True).then_inc(att_top_ready, 1)
                    if 1 <= st <= NT:
                        dve.wait_ge(pv_done, g * 8 + st)
                        by = att_inv[(st - 1) % 2][:, :].rearrange("p (e h) -> p h e", e=2)
                        dve.tensor_tensor(o_sb[:, :].rearrange("p (h e d) -> p h e d", h=2, e=2),
                                          ps[:, 4, 0:HG * DK].rearrange("p (h e d) -> p h e d", h=2, e=2),
                                          by.unsqueeze(3).broadcast_to([P, 2, 2, DK]), ALU.mult)\
                            .then_inc(o_ready, 1)
                    if st < NT:
                        dve.wait_ge(att_exp, g * 8 + (st + 1))
                        for b in range(BT):
                            q = slice(b * S, (b + 1) * S)
                            ins = dve.transpose(att_z[two][q, :, b * S:(b + 1) * S], att_p[two][q, :, :])
                        ins.then_inc(att_turned, 1)
                        mark(dve.reciprocal(att_inv[two][:, :], att_sum[two][:, :]))
                        settle()
                    if st >= 2:
                        dve.wait_ge(wo_done, g * 8 + (st - 1))
                        dve.wait_ge(wo_free, g * 8 + st)
                        for half in range(2):
                            part = x[:, st - 2, half * HALF:(half + 1) * HALF]
                            ins = dve.tensor_tensor(part, ps[:, (6, 2)[two] + half, :], part, ALU.add)
                        ins.then_inc(wo_free, 1)
                        if last:
                            dve.wait_ge(wo_free, g * 8 + (st + 1))
                            tile_stats(st - 2)
                    if last and st == NT:
                        normalise(2, 0)

            dve.wait_ge(z_zero, 2)
            dve.wait_ge(const_done, 5 + BT)
            start = own[0]
            base = at.base
            with dve.Fori(0, NG - 1) as g:
                at.base = g * GROUP_MARKS + base
                group(g)
                assert own[0] - start == GROUP_MARKS, own[0] - start
            at.base = base + GROUP_MARKS * (NG - 2)
            group(NG - 1, True)
            norm(2)

            def chunk(c, first=False):
                for k in range(2):
                    for half in range(2):
                        n = 2 * k + half
                        cols = slice(half * HALF, (half + 1) * HALF)
                        dve.wait_ge(silu_done, c * 4 + (n + 1))
                        dve.tensor_tensor(gf(half), sg(half), ps[:, 2 * n + 1, :], ALU.mult)\
                            .then_inc(h_done, 1)
                        dve.wait_ge(h_hi_done, c * 4 + (n + 1))
                        dve.tensor_tensor(h_lo[:, k, cols], gf(half), h_hi[:, k, cols].bitcast(F32),
                                          ALU.subtract).then_inc(h_ready, 1)
                for i in range(2 * NT):
                    t, half = i // 2, i % 2
                    part = x[:, t, half * HALF:(half + 1) * HALF]
                    dve.wait_ge(down_done, c * 16 + (i + 1))
                    if not first:
                        dve.wait_ge(down_added, (c - 1) * 16 + (i + 1))
                    dve.tensor_tensor(part, ps[:, i % 8, :], part, ALU.add).then_inc(down_added, 1)

            chunk(0, first=True)
            with dve.Fori(1, NC) as c:
                chunk(c)


TWO_TILE_MARKS = 18
GROUP_MARKS = 8


def flat(ap):
    n = len(ap.shape)
    names = "abcd"[:n - 1]
    return ap if n == 2 else ap.rearrange(f"p {' '.join(names)} -> p ({' '.join(names)})")


def flat3(t):
    return t[:, :, :, :].rearrange("p a b c -> p (a b c)")


def tile_psum(ps, bank):
    return ps[:, bank:bank + 2, :].rearrange("p e (k n) -> p (e k) n", n=P)


def blocks(padded):
    return padded[:, :].rearrange("p (b r) -> p b r", b=BT)[:, :, 0:MB]\
        .rearrange("p b (m n) -> p b m n", n=P)[:, :, :, 0:S]


def turned_psum(ps):
    return ps[:, 5, 0:MB].rearrange("p (m b n) -> p b m n", m=MT, b=BT)


def kernel(x, ctx_2048, mask_BxS2_bk0, L0_attn_Wq, L0_attn_Wk, L0_attn_Wv, L0_attn_Wo,
           L0_ffn_w_gate, L0_ffn_w_up, L0_ffn_w_down):
    import numpy as np
    import concourse.bacc as bacc
    from concourse.bass_utils import run_bass_kernel_spmd

    ctx, msk = np.asarray(ctx_2048), np.asarray(mask_BxS2_bk0)

    rows = ctx[:, :MB].reshape(B, MT, P, D).transpose(0, 2, 1, 3).reshape(B, P, UNIT)
    turned = ctx[:, :MB].transpose(0, 2, 1).reshape(B, KD, P, MB).transpose(0, 2, 1, 3).reshape(B, P, UNIT)
    order = [turned[b] for b in range(BT)]
    for t in range(NT):
        if t:
            order += [rows[(t - 1) * BT + b] for b in (2, 3)]
        if t + 1 < NT:
            order += [turned[(t + 1) * BT + b] for b in (0, 1)]
        order += [rows[t * BT + b] for b in (0, 1)]
        if t + 1 < NT:
            order += [turned[(t + 1) * BT + b] for b in (2, 3)]
    order += [rows[(NT - 1) * BT + b] for b in (2, 3)]

    def tiles_of(w, first, n):
        part = np.asarray(w)[first * P:(first + n) * P]
        return part.reshape(n, P, KD, P).transpose(3, 0, 2, 1).reshape(P, -1)

    def moving(w, first, n):
        part = np.asarray(w)[first * P:(first + n) * P]
        return part.reshape(n * P, KD, P).transpose(2, 1, 0).reshape(P, -1)

    def by_input(w, first, n):
        part = np.asarray(w)[:, first * P:(first + n) * P]
        return part.reshape(D, n, P).transpose(2, 1, 0).reshape(P, -1)

    pairs = []
    for g in range(NG):
        pairs += [tiles_of(L0_attn_Wq, g * FT, FT), tiles_of(L0_attn_Wk, g * FT, FT),
                  moving(L0_attn_Wv, g * FT, FT), by_input(L0_attn_Wo, g * FT, FT)]
    for c in range(NC):
        for j in (2 * c, 2 * c + 1):
            pairs.append(np.concatenate([tiles_of(L0_ffn_w_gate, j, 1), tiles_of(L0_ffn_w_up, j, 1)], 1))
        pairs.append(by_input(L0_ffn_w_down, 2 * c, 2))

    by_token = np.zeros((B, S, MC), msk.dtype)
    by_token[:, :, :MB] = msk[:, None, :MB]
    for b in range(B):
        by_token[b, :, MB + b] = msk[b, MB]
    arrays = {
        "x": np.ascontiguousarray(np.asarray(x).reshape(NT, P, D).transpose(1, 0, 2)),
        "ctx": np.ascontiguousarray(np.stack(order)),
        "w": np.ascontiguousarray(np.stack(pairs)),
        "mask": np.ascontiguousarray(by_token.reshape(NT, P, MC).transpose(1, 0, 2)),
        "ext": np.ascontiguousarray(ctx[:, MB]),
        "ext_t": np.ascontiguousarray(ctx[:, MB].T.reshape(KD, P, B).transpose(1, 0, 2).reshape(P, KD * B)),
    }
    nc = bacc.Bacc("TRN2", target_bir_lowering=False, num_devices=1)
    args = [nc.dram_tensor(f"in_{n}", arr.shape, mybir.dt.from_np(arr.dtype), kind="ExternalInput").ap()
            for n, arr in arrays.items()]
    out = nc.dram_tensor("out", (B * S, D), F32, kind="ExternalOutput").ap()
    build(nc, *args, out)
    r = run_bass_kernel_spmd(nc, [{f"in_{n}": arr for n, arr in arrays.items()}], core_ids=[0])
    return r.results[0]["out"].reshape(B, S, D)
```

```python
from contextlib import ExitStack

import concourse.bass as bass
from concourse import mybir

ALU = mybir.AluOpType
ACT = mybir.ActivationFunctionType
AX = mybir.AxisListType
F32 = mybir.dt.float32
F32R = mybir.dt.float32r
U8 = mybir.dt.uint8

P = 128
B, S, D, M = 32, 32, 1024, 257
MB = M // P * P
MT = MB // P
NT = B * S // P
BT = P // S
KD = D // P
HALF = 512
UNIT = 2048
H, DK = 16, 64
HG = 4
NG = H // HG
FT = HG * DK // P
DH = 4096
NC = DH // 256
SLOTS = 4
MC = MB + B
EXT = MB + P
PTW = MB + S
BIG = 1e30
CAUSAL_FILL = -3e38
EPS = 1e-5
CTX_UNITS = 2 * B
ATT_PAIRS = 4 * NG
CTX_USES = CTX_UNITS // SLOTS
ATT_USES = CTX_USES + ATT_PAIRS // SLOTS
FFN_SLOTS = 3


def build(nc, x_in, ctx_in, w_in, mask_in, ext_in, ext_t_in, out):
    stack = ExitStack()
    with stack:
        def sb(where, name, shape, dt=F32):
            return where.enter_context(nc.sbuf_tensor(name, shape, dt))

        def sem(name):
            return stack.enter_context(nc.semaphore(name))

        x = sb(stack, "x", [P, NT, D])
        raw = [sb(stack, f"raw{i}", [P, UNIT]) for i in range(SLOTS)]
        xn = [sb(stack, f"xn{i}", [P, D]) for i in range(2)]
        ident = sb(stack, "ident", [P, P])
        causal = sb(stack, "causal", [P, S])
        stats = sb(stack, "stats", [P, 2, 6])
        stats_next = sb(stack, "stats_next", [P, 2, 6])
        mean_var = sb(stack, "mean_var", [P, NT, 2])
        mean_var_now = sb(stack, "mean_var_now", [P, 2])
        rstd = sb(stack, "rstd", [P, NT, 1])
        mean_var_next = sb(stack, "mean_var_next", [P, 2])
        var_next = sb(stack, "var_next", [P, 1])
        rstd_next = sb(stack, "rstd_next", [P, 1])
        shift = sb(stack, "shift", [P, NT, 1])
        minus_half = sb(stack, "minus_half", [P, NT])

        a = ExitStack()
        cT_hi = [sb(a, f"cT_hi{i}", [P, 2, KD, MB], F32R) for i in range(2)]
        cT_lo = [sb(a, f"cT_lo{i}", [P, 2, KD, MB], F32R) for i in range(2)]
        cN_hi = [sb(a, f"cN_hi{i}", [P, MT, D], F32R) for i in range(2)]
        cN_lo = [sb(a, f"cN_lo{i}", [P, MT, D], F32R) for i in range(2)]
        xt_hi = sb(a, "xt_hi", [P, KD, P], F32R)
        xt_lo = sb(a, "xt_lo", [P, KD, P], F32R)
        pz_hi = sb(a, "pz_hi", [P, BT * PTW], F32R)
        pz_lo = sb(a, "pz_lo", [P, BT * PTW], F32R)
        p_ext = sb(a, "p_ext", [3 * B, P], F32R)
        ext = sb(a, "ext", [3 * B, D], F32R)
        extT = sb(a, "extT", [P, KD, 2, B], F32R)
        mask = sb(a, "mask", [P, NT, MC], U8)
        valid = sb(a, "valid", [P, NT, 1])
        fill = sb(a, "fill", [P, MC])
        sc_sb = sb(a, "sc_sb", [P, MC])
        prob = sb(a, "prob", [P, MC + 2 * B])
        neg_top = sb(a, "neg_top", [P, 1])
        total = sb(a, "total", [P, 1])
        inv = sb(a, "inv", [P, 1])
        inv_valid = [sb(a, f"inv_valid{i}", [P, 1]) for i in range(2)]
        a.close()

        w_hi = [sb(stack, f"w_hi{i}", [P, UNIT], F32R) for i in range(2)]
        w_lo = [sb(stack, f"w_lo{i}", [P, UNIT], F32R) for i in range(2)]
        xT_hi = sb(stack, "xT_hi", [P, KD, NT * P], F32R)
        xT_lo = sb(stack, "xT_lo", [P, KD, NT * P], F32R)
        s = ExitStack()
        qT = sb(s, "qT", [P, FT, NT * P])
        kT = sb(s, "kT", [P, FT, NT * P])
        v = sb(s, "v", [P, NT, HG * DK])
        att = [sb(s, f"att{i}", [P, 2, 2, S]) for i in range(2)]
        att_p = [sb(s, f"att_p{i}", [P, HG, S]) for i in range(2)]
        att_z = [sb(s, f"att_z{i}", [P, HG, P]) for i in range(2)]
        att_neg = [sb(s, f"att_neg{i}", [P, HG]) for i in range(2)]
        att_sum = [sb(s, f"att_sum{i}", [P, HG]) for i in range(2)]
        att_inv = [sb(s, f"att_inv{i}", [P, HG]) for i in range(2)]
        inv_once = sb(s, "inv_once", [P, 1])
        o_sb = sb(s, "o_sb", [P, HG * DK])
        oT_hi = sb(s, "oT_hi", [P, FT, P], F32R)
        oT_lo = sb(s, "oT_lo", [P, FT, P], F32R)
        s.close()
        w_hi.append(sb(stack, "w_hi2", [P, UNIT], F32R))
        w_lo.append(sb(stack, "w_lo2", [P, UNIT], F32R))
        h_hi = sb(stack, "h_hi", [P, 2, NT * P], F32R)
        h_lo = sb(stack, "h_lo", [P, 2, NT * P], F32R)

        ps = stack.enter_context(nc.psum_tensor("ps", [P, 8, HALF], F32))

        x_full = [sem(f"x_full{i}") for i in range(2)]
        mask_full = sem("mask_full")
        ext_full = sem("ext_full")
        ext_t_full = sem("ext_t_full")
        stored = sem("stored")
        raw_full = [sem(f"raw_full{i}") for i in range(SLOTS)]
        split_done = [sem(f"split_done{i}") for i in range(SLOTS)]
        hi_done = sem("hi_done")
        const_done = sem("const_done")
        dve_own = sem("dve_own")
        ext_hi_done = sem("ext_hi_done")
        ext_done = sem("ext_done")
        next_var_ready = sem("next_var_ready")
        next_scale_ready = sem("next_scale_ready")
        var_ready = sem("var_ready")
        pow_done = sem("pow_done")
        mean_scaled = sem("mean_scaled")
        scale_ready = sem("scale_ready")
        xn_ready = sem("xn_ready")
        xn_odd_ready = sem("xn_odd_ready")
        xt_psum = sem("xt_psum")
        xt_hi_done = sem("xt_hi_done")
        xt_ready = sem("xt_ready")
        scores_done = sem("scores_done")
        scores_read = sem("scores_read")
        top_ready = sem("top_ready")
        exp_done = sem("exp_done")
        pt_psum = sem("pt_psum")
        pt_hi_done = sem("pt_hi_done")
        pt_ready = sem("pt_ready")
        ctx_used = sem("ctx_used")
        readout_done = sem("readout_done")
        readout_free = sem("readout_free")
        q_done = sem("q_done")
        k_done = sem("k_done")
        v_done = sem("v_done")
        q_kept = sem("q_kept")
        k_kept = sem("k_kept")
        v_kept = sem("v_kept")
        att_done = sem("att_done")
        att_read = sem("att_read")
        att_top_ready = sem("att_top_ready")
        att_exp = sem("att_exp")
        att_turned = sem("att_turned")
        z_zero = sem("z_zero")
        pv_done = sem("pv_done")
        o_ready = sem("o_ready")
        oT_psum = sem("oT_psum")
        oT_hi_done = sem("oT_hi_done")
        oT_ready = sem("oT_ready")
        wo_done = sem("wo_done")
        wo_free = sem("wo_free")
        gu_done = sem("gu_done")
        silu_done = sem("silu_done")
        h_done = sem("h_done")
        h_hi_done = sem("h_hi_done")
        h_ready = sem("h_ready")
        down_done = sem("down_done")
        down_added = sem("down_added")

        def sg(half):
            return xn[0][:, half * HALF:(half + 1) * HALF]

        def gf(half):
            return xn[1][:, half * HALF:(half + 1) * HALF]

        block = stack.enter_context(nc.Block())

        def turned_unit(t, b):
            if isinstance(t, int) and t == 0:
                return b, b, 0
            return (t * 8 + (b - 4), b, t * 2 - 1) if b < 2 else (t * 8 + (b - 2), b - 2, t * 2)

        def rows_unit(t, b):
            if isinstance(t, int) and t == NT - 1:
                return CTX_UNITS - 4 + b, b, CTX_USES - 1
            return (t * 8 + (6 + b), 2 + b, t * 2 + 1) if b < 2 else (t * 8 + (8 + b), b, t * 2 + 2)

        def scales_of(n, t):
            return (n - 1) * NT + max(t + 1, NT - 2 if n == 1 else 0)

        TURN_BANKS = {1: (0, 6, 4, 2, 6, 4, 6, 4), 2: (2, 2, 2, 2, 2, 2, 2, 6)}
        TURN_AFTER = {1: (None, None, None, None, 1, 2, 4, 5), 2: (None, 0, 1, 2, 3, 4, 5, None)}
        Q_BANKS = (0, 1, 4, 5)
        K_BANKS = (2, 3, 6, 7)
        TURNED_HEADS = slice(HG * DK, HG * DK + FT * P)

        @block.sync
        def _(sync):
            sync.dma_start(x[:, 0, :], x_in[:, 0, :]).then_inc(x_full[0], 16)
            for i in range(SLOTS):
                sync.dma_start(raw[i][:, :], ctx_in[i]).then_inc(raw_full[i], 16)
            with sync.Fori(1, CTX_USES) as u:
                for i in range(SLOTS):
                    sync.wait_ge(split_done[i], u)
                    sync.dma_start(raw[i][:, :], ctx_in[u * SLOTS + i]).then_inc(raw_full[i], 16)
            with sync.Fori(0, NG) as g:
                for i in range(SLOTS):
                    sync.wait_ge(split_done[i], g + CTX_USES)
                    sync.dma_start(raw[i][:, :], w_in[g * SLOTS + i]).then_inc(raw_full[i], 16)
            with sync.Fori(0, NC) as c:
                for i in range(FFN_SLOTS):
                    sync.wait_ge(split_done[i], c + ATT_USES)
                    sync.dma_start(raw[i][:, :], w_in[c * FFN_SLOTS + (ATT_PAIRS + i)])\
                        .then_inc(raw_full[i], 16)
            for t in range(NT):
                sync.wait_ge(down_added, 2 * NT * (NC - 1) + 2 * t + 2)
                sync.dma_start(out[t * P:(t + 1) * P, :], x[:, t, :]).then_inc(stored, 16)
            sync.wait_ge(stored, 16 * NT)

        @block.gpsimd
        def _(pool):
            pool.dma_start(mask[:, :, :], mask_in).then_inc(mask_full, 16)
            pool.memset(ident[:, :], 0.0).then_inc(const_done, 1)
            pool.memset(causal[:, :], 0.0).then_inc(const_done, 1)
            pool.memset(minus_half[:, :], -0.5)
            pool.memset(pz_hi[:, :].bitcast(F32), 0.0).then_inc(const_done, 1)
            pool.memset(pz_lo[:, :].bitcast(F32), 0.0).then_inc(const_done, 1)
            pool.wait_ge(const_done, 4)
            pool.affine_select(out=ident[:, :], in_=ident[:, :], compare_op=ALU.not_equal, fill=1.0,
                               base=0, pattern=[[-1, P]], channel_multiplier=1).then_inc(const_done, 1)
            for b in range(BT):
                q = slice(b * S, (b + 1) * S)
                pool.wait_ge(const_done, 5 + b)
                pool.affine_select(out=causal[q, :], in_=causal[q, :], compare_op=ALU.is_ge,
                                   fill=CAUSAL_FILL, base=0, pattern=[[-1, S]],
                                   channel_multiplier=1).then_inc(const_done, 1)

            def lo(unit, dst, hi):
                n, slot, _ = unit
                pool.wait_ge(hi_done, n + 1)
                pool.tensor_tensor(dst, raw[slot][:, :], hi.bitcast(F32), ALU.subtract)\
                    .then_inc(split_done[slot], 1)

            def turned(t):
                lo(turned_unit(t, 3), flat(cT_lo[1][:, 1]), flat(cT_hi[1][:, 1]))

            def turned_second(t):
                lo(turned_unit(t, 1), flat(cT_lo[0][:, 1]), flat(cT_hi[0][:, 1]))

            def rows(t):
                lo(rows_unit(t, 3), flat(cN_lo[1][:, :, :]), flat(cN_hi[1][:, :, :]))

            def next_scale(t):
                pool.wait_ge(next_var_ready, t + 1)
                pool.tensor_tensor(rstd_next[:, :], var_next[:, :], minus_half[:, 0:1], ALU.pow)\
                    .then_inc(next_scale_ready, 1)

            def scales(n, t, tiles=1):
                part = slice(t + 1 - tiles, t + 1)
                count = (n - 1) * NT + t + 1
                pool.wait_ge(var_ready, count)
                pool.tensor_tensor(rstd[:, part, 0], mean_var[:, part, 1],
                                   minus_half[:, 0:tiles], ALU.pow).then_inc(pow_done, tiles)
                pool.wait_ge(pow_done, count)
                pool.tensor_tensor(shift[:, part, 0], mean_var[:, part, 0], rstd[:, part, 0], ALU.mult)\
                    .then_inc(mean_scaled, tiles)
                pool.wait_ge(mean_scaled, count)
                pool.tensor_scalar(shift[:, part, 0], shift[:, part, 0], -1.0, 1.0, ALU.mult, ALU.mult)\
                    .then_inc(scale_ready, tiles)

            pool.wait_ge(const_done, 5 + BT)
            next_scale(0)
            next_scale(1)
            turned_second(1)
            turned(1)
            next_scale(2)
            rows(0)
            turned_second(2)
            with pool.Fori(2, NT - 1) as t:
                turned(t)
                next_scale(t + 1)
                rows(t - 1)
                turned_second(t + 1)
            turned(NT - 1)
            rows(NT - 2)
            scales(1, NT - 3, NT - 2)

            def weights(slot, pair, wslot):
                pool.wait_ge(hi_done, pair + (CTX_UNITS + 1))
                pool.tensor_tensor(w_lo[wslot][:, :], raw[slot][:, :], w_hi[wslot][:, :].bitcast(F32),
                                   ALU.subtract).then_inc(split_done[slot], 1)

            weights(0, 0, 0)
            scales(1, NT - 2)
            scales(1, NT - 1)
            pool.wait_ge(wo_free, 1)
            for i in range(2):
                pool.memset(att_z[i][:, :, :], 0.0).then_inc(z_zero, 1)
            with pool.Fori(0, NG - 1) as g:
                for i in range(SLOTS):
                    weights((i + 1) % SLOTS, g * SLOTS + (i + 1), (i + 1) % 2)
            for i in range(1, SLOTS):
                weights(i, (NG - 1) * SLOTS + i, i % 2)
            for t in range(4):
                scales(2, t)
            weights(0, ATT_PAIRS, 0)
            for t in range(4, NT):
                scales(2, t)
            for i in (2, 3):
                weights(i % FFN_SLOTS, ATT_PAIRS + i, i % FFN_SLOTS)
            with pool.Fori(1, NC - 1) as c:
                for i in range(FFN_SLOTS):
                    k = (i + 1) % FFN_SLOTS
                    weights(k, c * FFN_SLOTS + (ATT_PAIRS + i + 1), k)
            for i in (1, 2):
                weights(i, (NC - 1) * FFN_SLOTS + ATT_PAIRS + i, i)

        @block.scalar
        def _(act):
            act.dma_start(prob[:, 0:KD * B], ext_t_in).then_inc(ext_t_full, 16)

            def hi(unit, dst):
                _, slot, use = unit
                act.wait_ge(raw_full[slot], (use + 1) * 16)
                act.activation(dst, raw[slot][:, :], ACT.Copy).then_inc(hi_done, 1)

            def turned(t, b):
                hi(turned_unit(t, b), flat(cT_hi[b // 2][:, b % 2]))

            def rows(t, b):
                hi(rows_unit(t, b), flat(cN_hi[b % 2][:, :, :]))

            act.wait_ge(ext_t_full, 16)
            act.activation(extT[:, :, 0, :], prob[:, 0:KD * B].rearrange("p (k b) -> p k b", b=B), ACT.Copy)\
                .then_inc(ext_hi_done, 1)
            turned(0, 0)

            def normalise(n, t):
                act.wait_ge(scale_ready, scales_of(n, t))
                if t > 1:
                    act.wait_ge(xt_psum, n * NT + t - 1)
                act.activation(xn[1][:, :], x[:, t, :], ACT.Identity, bias=shift[:, t, :],
                               scale=rstd[:, t, :]).then_inc(xn_odd_ready, 1)

            def tile(t, parity, first=False, last=False):
                if not last:
                    act.dma_start(x[:, t + 1, :], x_in[:, t + 1, :]).then_inc(x_full[1 - parity], 16)
                if first:
                    for i in range(3):
                        act.dma_start(xn[1][i * B:(i + 1) * B, :], ext_in).then_inc(ext_full, 16)
                act.wait_ge(xt_psum, t + 1)
                act.activation(flat(xt_hi[:, :, :]), flat(ps[:, 0:2, :]), ACT.Copy).then_inc(xt_hi_done, 1)
                if first:
                    for b in range(1, BT):
                        turned(0, b)
                    act.wait_ge(ext_full, 3 * 16)
                    act.activation(ext[:, :], xn[1][0:3 * B, :], ACT.Copy).then_inc(ext_hi_done, 1)
                else:
                    act.wait_ge(scores_done, t * 2)
                    turned(t, 2)
                    turned(t, 3)
                    for b in (2, 3):
                        act.wait_ge(ctx_used, t * 4 + (b - 5))
                        rows(t - 1, b)
                if not last:
                    act.wait_ge(scores_done, t * 2 + 1)
                    turned(t + 1, 0)
                    turned(t + 1, 1)
                if not first:
                    act.wait_ge(ctx_used, t * 4 - 1)
                rows(t, 0)
                act.wait_ge(top_ready, t + 1)
                act.activation(prob[:, MC:].rearrange("p (e b) -> p e b", b=B),
                               sc_sb[:, MB:MC].unsqueeze(1).broadcast_to([P, 2, B]), ACT.Exp,
                               bias=neg_top[:, 0:1])
                act.activation(prob[:, 0:MC], sc_sb[:, :], ACT.Exp, bias=neg_top[:, 0:1],
                               accum_out=total[:, 0:1]).then_inc(exp_done, 1)
                act.wait_ge(pt_psum, t + 1)
                if first:
                    act.wait_ge(const_done, 4)
                act.activation(blocks(pz_hi), turned_psum(ps), ACT.Copy)
                act.activation(p_ext[:, :], ps[0:3 * B, 5, MB:MB + P], ACT.Copy).then_inc(pt_hi_done, 1)
                if not first:
                    act.wait_ge(ctx_used, t * 4)
                rows(t, 1)

            tile(0, 0, first=True)
            tile(1, 1)
            with act.Fori(2, NT - 2, 2) as t:
                for parity in range(2):
                    tile(t + parity, parity)
            tile(NT - 2, 0)
            tile(NT - 1, 1, last=True)
            normalise(1, 1)
            for b in (2, 3):
                act.wait_ge(ctx_used, 4 * (NT - 1) + b - 1)
                rows(NT - 1, b)

            def weights(slot, use, wslot):
                act.wait_ge(raw_full[slot], (use + 1) * 16)
                act.activation(w_hi[wslot][:, :], raw[slot][:, :], ACT.Copy).then_inc(hi_done, 1)

            def pair_split(g, n):
                weights(n % 4, g + (CTX_USES + n // 4), n % 2)

            act.wait_ge(scores_done, 2 * NT)
            def turned_hi(n, t):
                act.wait_ge(xt_psum, n * NT + t + 1)
                act.activation(xT_hi[:, :, t * P:(t + 1) * P], tile_psum(ps, TURN_BANKS[n][t]), ACT.Copy)\
                    .then_inc(xt_hi_done, 1)

            pair_split(0, 0)
            for t in range(NT):
                turned_hi(1, t)
                if t % 2 and t + 2 < NT:
                    normalise(1, t + 2)
            pair_split(0, 1)

            def keep_queries(g, j):
                act.wait_ge(q_done, g * 4 + (j + 1))
                act.activation(qT[:, j % 2, (j // 2) * HALF:(j // 2 + 1) * HALF],
                               ps[:, Q_BANKS[j], :], ACT.Copy, scale=DK ** -0.5).then_inc(q_kept, 1)

            def group(g, last=False):
                def exps(st):
                    act.wait_ge(att_top_ready, g * 8 + (st + 1))
                    rowsof = flat3(att[st % 2])
                    for h in range(HG):
                        ins = act.activation(att_p[st % 2][:, h, :], rowsof[:, h * S:(h + 1) * S], ACT.Exp,
                                             bias=att_neg[st % 2][:, h:h + 1],
                                             accum_out=att_sum[st % 2][:, h:h + 1])
                    ins.then_inc(att_exp, 1)

                def keep_values(t):
                    act.wait_ge(v_done, g * 8 + (t + 1))
                    act.activation(v[:, t, :], ps[:, 5, 0:HG * DK], ACT.Copy).then_inc(v_kept, 1)

                keep_queries(g, 2)
                keep_queries(g, 3)
                pair_split(g, 2)
                act.wait_ge(k_done, g * 4 + 4)
                pair_split(g, 3)
                keep_values(0)
                for st in range(NT + 2):
                    if st >= 2:
                        act.wait_ge(oT_psum, g * 8 + (st - 1))
                        act.activation(flat(oT_hi[:, :, :]), ps[:, 4, TURNED_HEADS], ACT.Copy)\
                            .then_inc(oT_hi_done, 1)
                    if last and st >= 4:
                        turned_hi(2, st - 4)
                    if st < NT:
                        exps(st)
                    if st + 1 < NT:
                        keep_values(st + 1)
                    if last and st % 2 == 0 and st >= 4:
                        normalise(2, st - 3)
                    if st + 1 == NT - 1:
                        pair_split(g, 4)
                if not last:
                    keep_queries(g + 1, 0)
                    act.wait_ge(wo_done, (g + 1) * NT)
                    pair_split(g, 5)
                    keep_queries(g + 1, 1)

            keep_queries(0, 0)
            keep_queries(0, 1)
            with act.Fori(0, NG - 1) as g:
                group(g)
            group(NG - 1, last=True)
            act.wait_ge(wo_done, NG * NT)
            pair_split(NG - 1, 5)
            turned_hi(2, NT - 2)
            normalise(2, NT - 1)
            turned_hi(2, NT - 1)

            def chunk(c, first=False, last=False):
                for k in range(3):
                    if not (first and k == 0) and not (last and k == 2):
                        if k == 0:
                            act.wait_ge(gu_done, c * 4)
                        elif k == 2:
                            act.wait_ge(gu_done, c * 4 + (3 if first else 2))
                        elif not first:
                            act.wait_ge(down_done, c * 16)
                        nxt = (k + 1) % 3
                        weights(nxt, c + (ATT_USES + (k + 1) // 3), nxt)
                    if k < 2:
                        for half in range(2):
                            n = 2 * k + half
                            act.wait_ge(gu_done, c * 4 + (3 if first and n == 1 else n + 1))
                            act.activation(sg(half), ps[:, 2 * n, :], ACT.Silu).then_inc(silu_done, 1)
                            act.wait_ge(h_done, c * 4 + (n + 1))
                            act.activation(h_hi[:, k, half * HALF:(half + 1) * HALF], gf(half), ACT.Copy)\
                                .then_inc(h_hi_done, 1)

            chunk(0, first=True)
            with act.Fori(1, NC - 1) as c:
                chunk(c)
            chunk(NC - 1, last=True)

        @block.tensor
        def _(pe):
            def three(dst, stat, moving, start, stop):
                pe.matmul(dst, stat[0], moving[0], start=start, stop=False)
                pe.matmul(dst, stat[0], moving[1], start=False, stop=False)
                return pe.matmul(dst, stat[1], moving[0], start=False, stop=stop)

            def unit_ready(unit):
                _, slot, use = unit
                pe.wait_ge(split_done[slot], use + 1)

            def turn(src, banks):
                for k in range(KD):
                    mm = pe.transpose(ps[:, banks + k // 4, (k % 4) * P:(k % 4 + 1) * P],
                                      src[:, k * P:(k + 1) * P], ident[:, :])
                mm.then_inc(xt_psum, 1)

            def readout(t, parity, batches):
                bank = (6, 2)[parity]
                for b in batches:
                    unit_ready(rows_unit(t, b))
                    for half in range(2):
                        for m in range(MT):
                            col = b * MB + m * P
                            mm = three(ps[:, bank + half, :],
                                       (pz_hi[:, col:col + P], pz_lo[:, col:col + P]),
                                       (cN_hi[b % 2][:, m, half * HALF:(half + 1) * HALF],
                                        cN_lo[b % 2][:, m, half * HALF:(half + 1) * HALF]),
                                       start=(b == 0 and m == 0), stop=False)
                    mm.then_inc(ctx_used, 1)
                if 3 in batches:
                    if isinstance(t, int) and t == 0:
                        pe.wait_ge(ext_done, 2)
                    for half in range(2):
                        mm = pe.matmul(ps[:, bank + half, :], p_ext[:, :],
                                       ext[:, half * HALF:(half + 1) * HALF], start=False, stop=True)
                    mm.then_inc(readout_done, 1)

            def tile(t, parity, first=False):
                pe.wait_ge(xn_ready, t + 1)
                if not first:
                    pe.wait_ge(scores_read, t)
                turn(xn[0], 0)
                if not first:
                    pe.wait_ge(pt_ready, t)
                    pe.wait_ge(readout_free, t)
                    readout(t - 1, 1 - parity, (0, 1))
                pe.wait_ge(xt_ready, t + 1)
                if first:
                    pe.wait_ge(ext_done, 1)
                for k in range(KD):
                    pe.matmul(ps[:, 5, EXT:EXT + 2 * B], xt_hi[:, k, :],
                              extT[:, k, :, :].rearrange("p e b -> p (e b)"), start=(k == 0), stop=False)
                    pe.matmul(ps[:, 5, EXT:EXT + B], xt_lo[:, k, :], extT[:, k, 0, :], start=False,
                              stop=(k == KD - 1))
                for pair in range(2):
                    for b in (2 * pair, 2 * pair + 1):
                        unit_ready(turned_unit(t, b))
                    for k in range(KD):
                        mm = three(ps[:, pair, :].rearrange("p (b m) -> p b m", b=2),
                                   (xt_hi[:, k, :], xt_lo[:, k, :]),
                                   (cT_hi[pair][:, :, k, :], cT_lo[pair][:, :, k, :]),
                                   start=(k == 0), stop=(k == KD - 1))
                    mm.then_inc(scores_done, 1)
                if not first:
                    readout(t - 1, 1 - parity, (2, 3))
                pe.wait_ge(exp_done, t + 1)
                for m in range(MT):
                    pe.transpose(ps[:, 5, m * P:(m + 1) * P], prob[:, m * P:(m + 1) * P], ident[:, :])
                pe.transpose(ps[0:3 * B, 5, MB:MB + P], prob[:, MB:], ident[:, :]).then_inc(pt_psum, 1)

            pe.wait_ge(const_done, 5)
            tile(0, 0, first=True)
            tile(1, 1)
            with pe.Fori(2, NT - 2, 2) as t:
                for parity in range(2):
                    tile(t + parity, parity)
            tile(NT - 2, 0)
            tile(NT - 1, 1)

            def norm_tile(n, t):
                if t % 2:
                    pe.wait_ge(xn_odd_ready, (n - 1) * NT // 2 + t // 2 + 1)
                else:
                    pe.wait_ge(xn_ready, NT + (n - 1) * NT // 2 + t // 2 + 1)
                if TURN_AFTER[n][t] is not None:
                    pe.wait_ge(xt_ready, n * NT + TURN_AFTER[n][t] + 1)
                turn(xn[t % 2], TURN_BANKS[n][t])

            pe.wait_ge(pt_ready, NT)
            pe.wait_ge(readout_free, NT)
            readout(NT - 1, 1, (0, 1))
            norm_tile(1, 0)
            pe.wait_ge(readout_free, NT + 1)
            norm_tile(1, 1)
            readout(NT - 1, 1, (2, 3))
            norm_tile(1, 2)
            pe.wait_ge(readout_free, NT + 2)
            norm_tile(1, 3)

            def stationary(slot, unit, k):
                at = (unit * KD + k) * P
                return w_hi[slot][:, at:at + P], w_lo[slot][:, at:at + P]

            def tokens(k, at, n):
                return xT_hi[:, k, at:at + n], xT_lo[:, k, at:at + n]

            def scores(g, st):
                for h in range(HG):
                    r = slice((h % 2) * DK, (h % 2 + 1) * DK)
                    mm = pe.matmul(ps[:, h % 2, (h // 2) * P:(h // 2 + 1) * P],
                                   qT[r, h // 2, st * P:(st + 1) * P],
                                   kT[r, h // 2, st * P:(st + 1) * P], start=True, stop=True)
                mm.then_inc(att_done, 1)

            def job(bank, pair, j, slices=range(KD), at=0, n=HALF):
                for k in slices:
                    mm = three(ps[:, bank, at:at + n], stationary(pair % 2, j % 2, k),
                               tokens(k, (j // 2) * HALF + at, n), start=(k == 0), stop=(k == KD - 1))
                return mm

            def group(g, last=False):
                for j in (2, 3):
                    job(Q_BANKS[j], 0, j).then_inc(q_done, 1)
                pe.wait_ge(split_done[1], g + (CTX_USES + 1))
                for j in range(2 * FT):
                    if j == 2:
                        pe.wait_ge(wo_free, g * 8 + 1)
                    job(K_BANKS[j], 1, j).then_inc(k_done, 1)
                pe.wait_ge(split_done[2], g + (CTX_USES + 1))

                def values(t):
                    W = HG * DK
                    if t == 0:
                        pe.wait_ge(q_kept, g * 4 + 4)
                    else:
                        pe.wait_ge(v_kept, g * 8 + t)
                    for k in range(KD):
                        mm = three(ps[:, 5, 0:W], tokens(k, t * P, P),
                                   (w_hi[0][:, k * W:(k + 1) * W], w_lo[0][:, k * W:(k + 1) * W]),
                                   start=(k == 0), stop=(k == KD - 1))
                    mm.then_inc(v_done, 1)

                def turn_heads(t):
                    pe.wait_ge(o_ready, g * 8 + (t + 1))
                    for f in range(FT):
                        mm = pe.transpose(ps[:, 4, (FT + f) * P:(FT + f + 1) * P],
                                          o_sb[:, f * P:(f + 1) * P], ident[:, :])
                    mm.then_inc(oT_psum, 1)

                def attend(t):
                    pe.wait_ge(att_turned, g * 8 + (t + 1))
                    if t == NT - 1:
                        pe.wait_ge(v_kept, g * 8 + (t + 1))
                    if t >= 1:
                        pe.wait_ge(oT_ready, g * 8 + t)
                    for h in range(HG):
                        mm = pe.matmul(ps[:, 4, h * DK:(h + 1) * DK],
                                       att_z[t % 2][:, (h % 2) * 2 + h // 2, :],
                                       v[:, t, h * DK:(h + 1) * DK], start=True, stop=True)
                    mm.then_inc(pv_done, 1)

                def project(t):
                    if t == 0:
                        pe.wait_ge(split_done[3], g + (CTX_USES + 1))
                    pe.wait_ge(oT_ready, g * 8 + (t + 1))
                    pe.wait_ge(wo_free, g * 8 + (t + 1))
                    for f in range(FT):
                        for half in range(2):
                            at = f * D + half * HALF
                            mm = three(ps[:, 6 + half, :], (oT_hi[:, f, :], oT_lo[:, f, :]),
                                       (w_hi[1][:, at:at + HALF], w_lo[1][:, at:at + HALF]),
                                       start=(f == 0), stop=(f == FT - 1))
                    mm.then_inc(wo_done, 1)

                values(0)
                pe.wait_ge(k_kept, g * 4 + 4)
                scores(g, 0)
                values(1)
                pe.wait_ge(att_read, g * 8 + 1)
                scores(g, 1)
                values(2)
                attend(0)
                for st in range(2, NT):
                    if st > 2:
                        turn_heads(st - 2)
                    pe.wait_ge(att_read, g * 8 + st)
                    scores(g, st)
                    if st == 2:
                        turn_heads(0)
                    if st < NT - 1:
                        values(st + 1)
                        attend(st - 1)
                        project(st - 2)
                    else:
                        project(st - 2)
                        attend(st - 1)
                    if last and st >= 3:
                        norm_tile(2, st - 3)
                pe.wait_ge(split_done[0], g + (CTX_USES + 2))
                pe.wait_ge(att_read, (g + 1) * 8)
                if last:
                    pe.wait_ge(xt_ready, 2 * NT + 4)
                job(0, 0, 0, range(0, 4))
                turn_heads(NT - 2)
                mm = job(0, 0, 0, range(4, KD))
                if not last:
                    mm.then_inc(q_done, 1)
                attend(NT - 1)
                project(NT - 2)
                if last:
                    norm_tile(2, NT - 3)
                turn_heads(NT - 1)
                if last:
                    job(1, 0, 1, range(0, 3))
                else:
                    job(1, 0, 1).then_inc(q_done, 1)
                project(NT - 1)
                if last:
                    norm_tile(2, NT - 2)

            pe.wait_ge(split_done[0], CTX_USES + 1)
            pe.wait_ge(xt_ready, NT + 2)
            job(Q_BANKS[0], 0, 0, at=0, n=2 * P)
            pe.wait_ge(xt_ready, NT + 4)
            job(Q_BANKS[0], 0, 0, at=2 * P, n=2 * P).then_inc(q_done, 1)
            norm_tile(1, 4)
            norm_tile(1, 5)
            job(Q_BANKS[1], 0, 1, range(0, 3))
            norm_tile(1, 6)
            norm_tile(1, 7)
            job(Q_BANKS[1], 0, 1, range(3, KD)).then_inc(q_done, 1)
            pe.wait_ge(xt_ready, 2 * NT)
            with pe.Fori(0, NG - 1) as g:
                group(g)
            group(NG - 1, last=True)
            job(1, 0, 1, range(3, KD)).then_inc(gu_done, 1)
            def gate_up(c, k, half, first=False):
                n = 2 * k + half
                if not first:
                    pe.wait_ge(down_added, (c - 1) * 16 + (8 + 2 * n + 2))
                for u in range(2):
                    mm = job(2 * n + u, k, 2 * half + u)
                mm.then_inc(gu_done, 1)

            def down(c):
                pe.wait_ge(split_done[2], c + (ATT_USES + 1))
                for i in range(2 * NT):
                    t, half = i // 2, i % 2
                    if i == 0:
                        pe.wait_ge(h_ready, c * 4 + 3)
                    if i == NT:
                        pe.wait_ge(h_ready, c * 4 + 4)
                    if i < 8:
                        pe.wait_ge(h_done, c * 4 + (i // 2 + 1))
                    else:
                        pe.wait_ge(down_added, c * 16 + (i - 7))
                    for k in range(2):
                        at = k * D + half * HALF
                        mm = three(ps[:, i % 8, :],
                                   (h_hi[:, k, t * P:(t + 1) * P], h_lo[:, k, t * P:(t + 1) * P]),
                                   (w_hi[2][:, at:at + HALF], w_lo[2][:, at:at + HALF]),
                                   start=(k == 0), stop=(k == 1))
                    mm.then_inc(down_done, 1)

            pe.wait_ge(split_done[1], ATT_USES + 1)
            job(4, 1, 0)
            pe.wait_ge(wo_free, NG * NT + 1)
            norm_tile(2, NT - 1)
            job(5, 1, 1).then_inc(gu_done, 1)
            pe.wait_ge(xt_ready, 3 * NT)
            for k in range(2):
                gate_up(0, k, 1, first=True)
            down(0)
            with pe.Fori(1, NC) as c:
                for k in range(2):
                    pe.wait_ge(split_done[k], c + (ATT_USES + 1))
                    for half in range(2):
                        gate_up(c, k, half)
                down(c)

        @block.vector
        def _(dve):
            own = [0, 0]

            class at:
                base = 0

            def mark(ins):
                own[0] += 1
                ins.then_inc(dve_own, 1)

            def settle():
                dve.wait_ge(dve_own, at.base + own[0])

            def lo(unit, dst, hi):
                n, slot, _ = unit
                dve.wait_ge(hi_done, n + 1)
                dve.tensor_tensor(dst, raw[slot][:, :], hi.bitcast(F32), ALU.subtract)\
                    .then_inc(split_done[slot], 1)

            def turned(t, b):
                lo(turned_unit(t, b), flat(cT_lo[b // 2][:, b % 2]), flat(cT_hi[b // 2][:, b % 2]))

            def rows(t, b):
                lo(rows_unit(t, b), flat(cN_lo[b % 2][:, :, :]), flat(cN_hi[b % 2][:, :, :]))

            def both_stats(dst, t):
                for half in range(2):
                    ins = dve.bn_stats(dst[:, half, :], x[:, t, half * HALF:(half + 1) * HALF])
                mark(ins)

            def tile_stats(t):
                both_stats(stats, t)
                settle()
                mark(dve.bn_aggr(mean_var[:, t, :], stats[:, :, :]))
                settle()
                dve.tensor_scalar(mean_var[:, t, 1:2], mean_var[:, t, 1:2], EPS, None, ALU.add)\
                    .then_inc(var_ready, 1)

            def next_normalise(t):
                dve.wait_ge(next_scale_ready, t + 1)
                dve.tensor_scalar(xn[0][:, :], x[:, t, :], mean_var_next[:, 0:1], rstd_next[:, :],
                                  ALU.subtract, ALU.mult).then_inc(xn_ready, 1)

            def normalise(n, t):
                dve.wait_ge(scale_ready, scales_of(n, t))
                dve.tensor_scalar(xn[0][:, :], x[:, t, :], mean_var[:, t, 0:1], rstd[:, t, :],
                                  ALU.subtract, ALU.mult).then_inc(xn_ready, 1)

            dve.wait_ge(x_full[0], 16)
            both_stats(stats_next, 0)
            settle()
            mark(dve.bn_aggr(mean_var_next[:, :], stats_next[:, :, :]))
            settle()
            dve.tensor_scalar(var_next[:, :], mean_var_next[:, 1:2], EPS, None, ALU.add)\
                .then_inc(next_var_ready, 1)
            next_normalise(0)
            dve.wait_ge(ext_hi_done, 1)
            dve.tensor_tensor(extT[:, :, 1, :], prob[:, 0:KD * B].rearrange("p (k b) -> p k b", b=B),
                              extT[:, :, 0, :].bitcast(F32), ALU.subtract).then_inc(ext_done, 1)
            turned(0, 0)

            def add_readout(t, parity):
                dve.wait_ge(readout_done, t + 1)
                settle()
                for half in range(2):
                    part = x[:, t, half * HALF:(half + 1) * HALF]
                    ins = dve.scalar_tensor_tensor(out=part, in0=ps[:, (6, 2)[parity] + half, :],
                                                   scalar=inv_valid[parity][:, 0:1], in1=part,
                                                   op0=ALU.mult, op1=ALU.add)
                ins.then_inc(readout_free, 1)

            def tile(t, parity, early=False, first=False, last=False):
                dve.wait_ge(xt_hi_done, t + 1)
                dve.tensor_tensor(flat(xt_lo[:, :, :]), flat(ps[:, 0:2, :]),
                                  flat(xt_hi[:, :, :]).bitcast(F32), ALU.subtract).then_inc(xt_ready, 1)
                if first:
                    for b in range(1, BT):
                        turned(0, b)
                    dve.wait_ge(mask_full, 16)
                    dve.memset(inv_valid[1][:, :], 0.0).then_inc(readout_free, 2)
                if not first:
                    turned(t, 2)
                if not last:
                    dve.wait_ge(x_full[1 - parity], (t + (2 + parity)) * 8)
                mark(dve.tensor_scalar(fill[:, :], mask[:, t, :], BIG, -BIG, ALU.mult, ALU.add))
                if not last:
                    both_stats(stats_next, t + 1)
                settle()
                if not first:
                    rows(t - 1, 2)
                if not last:
                    mark(dve.bn_aggr(mean_var_next[:, :], stats_next[:, :, :]))
                if not early:
                    add_readout(t - 2, parity)
                settle()
                if not last:
                    dve.tensor_scalar(var_next[:, :], mean_var_next[:, 1:2], EPS, None, ALU.add)\
                        .then_inc(next_var_ready, 1)
                if first:
                    mark(dve.tensor_reduce(valid[:, :, 0], mask[:, :, :], AX.X, ALU.max))
                if not early:
                    dve.wait_ge(readout_free, t + 1)
                if not last:
                    next_normalise(t + 1)
                if not early:
                    both_stats(stats, t - 2)
                    settle()
                if not last:
                    turned(t + 1, 0)
                if first:
                    dve.wait_ge(ext_hi_done, 2)
                    low = slice(2 * B, 3 * B)
                    dve.tensor_tensor(ext[low, :], xn[1][low, :], ext[low, :].bitcast(F32), ALU.subtract)\
                        .then_inc(ext_done, 1)
                if not early:
                    mark(dve.bn_aggr(mean_var_now[:, :], stats[:, :, :]))
                    settle()
                    mark(dve.tensor_copy(mean_var[:, t - 2, :], mean_var_now[:, :]))
                if last:
                    settle()
                    dve.tensor_scalar(mean_var[:, 0:NT - 2, 1], mean_var[:, 0:NT - 2, 1], EPS, None,
                                      ALU.add).then_inc(var_ready, NT - 2)
                dve.wait_ge(scores_done, t * 2 + 2)
                for b in range(BT):
                    q = slice(b * S, (b + 1) * S)
                    dve.scalar_tensor_tensor(out=sc_sb[q, 0:MB],
                                             in0=ps[q, b // 2, (b % 2) * MB:(b % 2 + 1) * MB],
                                             scalar=D ** -0.5, in1=mask[q, t, 0:MB],
                                             op0=ALU.mult, op1=ALU.mult)
                dve.scalar_tensor_tensor(out=fill[:, MB:MC], in0=ps[:, 5, EXT + B:EXT + 2 * B],
                                         scalar=D ** -0.5, in1=fill[:, MB:MC], op0=ALU.mult,
                                         op1=ALU.add)
                dve.scalar_tensor_tensor(out=sc_sb[:, MB:MC], in0=ps[:, 5, EXT:EXT + B],
                                         scalar=D ** -0.5, in1=mask[:, t, MB:MC], op0=ALU.mult,
                                         op1=ALU.mult).then_inc(scores_read, 1)
                dve.wait_ge(scores_read, t + 1)
                settle()
                mark(dve.tensor_tensor(sc_sb[:, :], sc_sb[:, :], fill[:, :], ALU.add))
                settle()
                dve.tensor_reduce(neg_top[:, :], sc_sb[:, :], AX.X, ALU.max, negate=True)\
                    .then_inc(top_ready, 1)
                rows(t, 0)
                dve.wait_ge(exp_done, t + 1)
                mark(dve.reciprocal(inv[:, :], total[:, :]))
                settle()
                mark(dve.tensor_scalar(inv_valid[parity][:, :], inv[:, :], valid[:, t, :], None, ALU.mult))
                dve.wait_ge(pt_hi_done, t + 1)
                if first:
                    dve.wait_ge(const_done, 4)
                dve.tensor_tensor(blocks(pz_lo), turned_psum(ps), blocks(pz_hi).bitcast(F32), ALU.subtract)
                low = slice(B, 2 * B)
                dve.tensor_tensor(p_ext[low, :], ps[low, 5, MB:MB + P], p_ext[low, :].bitcast(F32),
                                  ALU.subtract).then_inc(pt_ready, 1)
                rows(t, 1)

            tile(0, 0, early=True, first=True)
            tile(1, 1, early=True)
            start = own[0]
            with dve.Fori(2, NT - 2, 2) as t:
                at.base = (t - 2) * (TWO_TILE_MARKS // 2)
                for parity in range(2):
                    tile(t + parity, parity)
                assert own[0] - start == TWO_TILE_MARKS, own[0] - start
            at.base = TWO_TILE_MARKS * ((NT - 4) // 2 - 1)
            tile(NT - 2, 0)
            tile(NT - 1, 1, last=True)

            def turned_lo(n, t):
                dve.wait_ge(xt_hi_done, n * NT + t + 1)
                dve.tensor_tensor(xT_lo[:, :, t * P:(t + 1) * P], tile_psum(ps, TURN_BANKS[n][t]),
                                  xT_hi[:, :, t * P:(t + 1) * P].bitcast(F32), ALU.subtract)\
                    .then_inc(xt_ready, 1)

            normalise(1, 0)
            add_readout(NT - 2, 0)
            rows(NT - 1, 2)
            rows(NT - 1, 3)
            dve.wait_ge(readout_free, NT + 1)
            tile_stats(NT - 2)
            dve.wait_ge(xt_psum, NT + 1)
            normalise(1, 2)
            add_readout(NT - 1, 1)
            for t in range(3):
                turned_lo(1, t)
            dve.wait_ge(readout_free, NT + 2)
            dve.memset(inv_once[:, :], 0.0).then_inc(wo_free, 1)
            turned_lo(1, 3)
            tile_stats(NT - 1)
            for t in (4, 6):
                dve.wait_ge(xt_psum, NT + t - 1)
                normalise(1, t)
                if t == 6:
                    turned_lo(1, 4)
                    turned_lo(1, 5)
            turned_lo(1, 6)
            turned_lo(1, 7)

            def group(g, last=False):
                for j in range(2 * FT):
                    dve.wait_ge(k_done, g * 4 + (j + 1))
                    dve.tensor_copy(kT[:, j % 2, (j // 2) * HALF:(j // 2 + 1) * HALF], ps[:, K_BANKS[j], :])\
                        .then_inc(k_kept, 1)
                for st in range(NT + 2):
                    two = st % 2
                    if st >= 2:
                        dve.wait_ge(oT_hi_done, g * 8 + (st - 1))
                        dve.tensor_tensor(flat(oT_lo[:, :, :]), ps[:, 4, TURNED_HEADS],
                                          flat(oT_hi[:, :, :]).bitcast(F32), ALU.subtract)\
                            .then_inc(oT_ready, 1)
                    if st < NT:
                        dve.wait_ge(att_done, g * 8 + (st + 1))
                        for b in range(BT):
                            q = slice(b * S, (b + 1) * S)
                            src = ps[q, 0:2, 0:2 * P].rearrange("p e (h k) -> p e h k", h=2)
                            ins = dve.tensor_tensor(
                                att[two][q, :, :, :], src[:, :, :, b * S:(b + 1) * S],
                                causal[q, :].unsqueeze(1).unsqueeze(1).broadcast_to([S, 2, 2, S]), ALU.add)
                        ins.then_inc(att_read, 1)
                        dve.wait_ge(att_read, g * 8 + (st + 1))
                        dve.tensor_reduce(att_neg[two][:, :],
                                          flat3(att[two]).rearrange("p (h k) -> p h k", h=HG), AX.X,
                                          ALU.max, negate=True).then_inc(att_top_ready, 1)
                    if last and st >= 4:
                        turned_lo(2, st - 4)
                    if st < NT:
                        dve.wait_ge(att_exp, g * 8 + (st + 1))
                        for b in range(BT):
                            q = slice(b * S, (b + 1) * S)
                            ins = dve.transpose(att_z[two][q, :, b * S:(b + 1) * S], att_p[two][q, :, :])
                        ins.then_inc(att_turned, 1)
                        mark(dve.reciprocal(att_inv[two][:, :], att_sum[two][:, :]))
                        settle()
                    if last and st % 2 and st >= 3:
                        if st > 3:
                            dve.wait_ge(xt_psum, 2 * NT + st - 4)
                        normalise(2, st - 3)
                    if 1 <= st <= NT:
                        dve.wait_ge(pv_done, g * 8 + st)
                        by = att_inv[(st - 1) % 2][:, :].rearrange("p (e h) -> p h e", e=2)
                        dve.tensor_tensor(o_sb[:, :].rearrange("p (h e d) -> p h e d", h=2, e=2),
                                          ps[:, 4, 0:HG * DK].rearrange("p (h e d) -> p h e d", h=2, e=2),
                                          by.unsqueeze(3).broadcast_to([P, 2, 2, DK]), ALU.mult)\
                            .then_inc(o_ready, 1)
                    if st >= 2:
                        dve.wait_ge(wo_done, g * 8 + (st - 1))
                        for half in range(2):
                            part = x[:, st - 2, half * HALF:(half + 1) * HALF]
                            ins = dve.tensor_tensor(part, ps[:, 6 + half, :], part, ALU.add)
                        ins.then_inc(wo_free, 1)
                        if last and st == NT + 1:
                            dve.wait_ge(hi_done, CTX_UNITS + ATT_PAIRS + 2)
                            dve.tensor_tensor(w_lo[1][:, :], raw[1][:, :], w_hi[1][:, :].bitcast(F32),
                                              ALU.subtract).then_inc(split_done[1], 1)
                        if last:
                            dve.wait_ge(wo_free, g * 8 + st)
                            tile_stats(st - 2)

            dve.wait_ge(z_zero, 2)
            dve.wait_ge(const_done, 5 + BT)
            start = own[0]
            base = at.base
            with dve.Fori(0, NG - 1) as g:
                at.base = g * GROUP_MARKS + base
                group(g)
                assert own[0] - start == GROUP_MARKS, own[0] - start
            at.base = base + GROUP_MARKS * (NG - 2)
            group(NG - 1, True)
            turned_lo(2, NT - 2)
            turned_lo(2, NT - 1)

            def chunk(c, first=False):
                for k in range(2):
                    for half in range(2):
                        n = 2 * k + half
                        cols = slice(half * HALF, (half + 1) * HALF)
                        dve.wait_ge(silu_done, c * 4 + (n + 1))
                        dve.tensor_tensor(gf(half), sg(half), ps[:, 2 * n + 1, :], ALU.mult)\
                            .then_inc(h_done, 1)
                        dve.wait_ge(h_hi_done, c * 4 + (n + 1))
                        dve.tensor_tensor(h_lo[:, k, cols], gf(half), h_hi[:, k, cols].bitcast(F32),
                                          ALU.subtract).then_inc(h_ready, 1)
                for i in range(2 * NT):
                    t, half = i // 2, i % 2
                    part = x[:, t, half * HALF:(half + 1) * HALF]
                    dve.wait_ge(down_done, c * 16 + (i + 1))
                    if not first:
                        dve.wait_ge(down_added, (c - 1) * 16 + (i + 1))
                    dve.tensor_tensor(part, ps[:, i % 8, :], part, ALU.add).then_inc(down_added, 1)

            chunk(0, first=True)
            with dve.Fori(1, NC) as c:
                chunk(c)


TWO_TILE_MARKS = 18
GROUP_MARKS = 8


def flat(ap):
    n = len(ap.shape)
    names = "abcd"[:n - 1]
    return ap if n == 2 else ap.rearrange(f"p {' '.join(names)} -> p ({' '.join(names)})")


def flat3(t):
    return t[:, :, :, :].rearrange("p a b c -> p (a b c)")


def tile_psum(ps, bank):
    return ps[:, bank:bank + 2, :].rearrange("p e (k n) -> p (e k) n", n=P)


def blocks(padded):
    return padded[:, :].rearrange("p (b r) -> p b r", b=BT)[:, :, 0:MB]\
        .rearrange("p b (m n) -> p b m n", n=P)[:, :, :, 0:S]


def turned_psum(ps):
    return ps[:, 5, 0:MB].rearrange("p (m b n) -> p b m n", m=MT, b=BT)


def kernel(x, ctx_2048, mask_BxS2_bk0, L0_attn_Wq, L0_attn_Wk, L0_attn_Wv, L0_attn_Wo,
           L0_ffn_w_gate, L0_ffn_w_up, L0_ffn_w_down):
    import numpy as np
    import concourse.bacc as bacc
    from concourse.bass_utils import run_bass_kernel_spmd

    ctx, msk = np.asarray(ctx_2048), np.asarray(mask_BxS2_bk0)

    rows = ctx[:, :MB].reshape(B, MT, P, D).transpose(0, 2, 1, 3).reshape(B, P, UNIT)
    turned = ctx[:, :MB].transpose(0, 2, 1).reshape(B, KD, P, MB).transpose(0, 2, 1, 3).reshape(B, P, UNIT)
    order = [turned[b] for b in range(BT)]
    for t in range(NT):
        if t:
            order += [rows[(t - 1) * BT + b] for b in (2, 3)]
        if t + 1 < NT:
            order += [turned[(t + 1) * BT + b] for b in (0, 1)]
        order += [rows[t * BT + b] for b in (0, 1)]
        if t + 1 < NT:
            order += [turned[(t + 1) * BT + b] for b in (2, 3)]
    order += [rows[(NT - 1) * BT + b] for b in (2, 3)]

    def tiles_of(w, first, n):
        part = np.asarray(w)[first * P:(first + n) * P]
        return part.reshape(n, P, KD, P).transpose(3, 0, 2, 1).reshape(P, -1)

    def moving(w, first, n):
        part = np.asarray(w)[first * P:(first + n) * P]
        return part.reshape(n * P, KD, P).transpose(2, 1, 0).reshape(P, -1)

    def by_input(w, first, n):
        part = np.asarray(w)[:, first * P:(first + n) * P]
        return part.reshape(D, n, P).transpose(2, 1, 0).reshape(P, -1)

    pairs = []
    for g in range(NG):
        pairs += [tiles_of(L0_attn_Wq, g * FT, FT), tiles_of(L0_attn_Wk, g * FT, FT),
                  moving(L0_attn_Wv, g * FT, FT), by_input(L0_attn_Wo, g * FT, FT)]
    for c in range(NC):
        for j in (2 * c, 2 * c + 1):
            pairs.append(np.concatenate([tiles_of(L0_ffn_w_gate, j, 1), tiles_of(L0_ffn_w_up, j, 1)], 1))
        pairs.append(by_input(L0_ffn_w_down, 2 * c, 2))

    by_token = np.zeros((B, S, MC), msk.dtype)
    by_token[:, :, :MB] = msk[:, None, :MB]
    for b in range(B):
        by_token[b, :, MB + b] = msk[b, MB]
    arrays = {
        "x": np.ascontiguousarray(np.asarray(x).reshape(NT, P, D).transpose(1, 0, 2)),
        "ctx": np.ascontiguousarray(np.stack(order)),
        "w": np.ascontiguousarray(np.stack(pairs)),
        "mask": np.ascontiguousarray(by_token.reshape(NT, P, MC).transpose(1, 0, 2)),
        "ext": np.ascontiguousarray(ctx[:, MB]),
        "ext_t": np.ascontiguousarray(ctx[:, MB].T.reshape(KD, P, B).transpose(1, 0, 2).reshape(P, KD * B)),
    }
    nc = bacc.Bacc("TRN2", target_bir_lowering=False, num_devices=1)
    args = [nc.dram_tensor(f"in_{n}", arr.shape, mybir.dt.from_np(arr.dtype), kind="ExternalInput").ap()
            for n, arr in arrays.items()]
    out = nc.dram_tensor("out", (B * S, D), F32, kind="ExternalOutput").ap()
    build(nc, *args, out)
    r = run_bass_kernel_spmd(nc, [{f"in_{n}": arr for n, arr in arrays.items()}], core_ids=[0])
    return r.results[0]["out"].reshape(B, S, D)
```
